# Optimizing a Trainium2 kernel written in Bass

```python
import numpy as np
import jax
import jax.numpy as jnp

def _softmax(x, axis=-1):
    return jax.nn.softmax(x, axis=axis)

def _gelu(x):
    return jax.nn.gelu(x, approximate=True)

def _silu(x):
    return jax.nn.silu(x)

def _sigmoid(x):
    return jax.nn.sigmoid(x)

def _layernorm(x, axis=-1, eps=1e-05):
    m = jnp.mean(x, axis=axis, keepdims=True)
    v = jnp.var(x, axis=axis, keepdims=True)
    return (x - m) / jnp.sqrt(v + eps)

def _scatter_add(tgt, idx, src, axis=0):
    return tgt.at[idx].add(src)

def _segment_sum(src, seg, n):
    return jax.ops.segment_sum(src, seg, n)
kernel_name = 'mk_xattn_ffn_d2_seqx_r8_c77094'

def setup_inputs(seed: int=0):
    np.random.seed(seed)
    _w = jnp.asarray

    def _rec_inputs():
        import jax
        import jax.numpy as jnp
        _rk = jax.random.key(seed)
        x = -0.000125 + 0.9999 * jax.random.normal(jax.random.fold_in(_rk, 1), (2, 256, 512), jnp.float32)
        _lenS = 256 - jax.random.randint(jax.random.fold_in(_rk, 7), (2,), 0, max(1, 256 // 4) + 1, jnp.int32)
        _lenS2 = 512 - jax.random.randint(jax.random.fold_in(_rk, 8), (2,), 0, max(1, 512 // 4) + 1, jnp.int32)
        _ctx_4096P = jax.random.normal(jax.random.fold_in(_rk, 11), (2, 16, 512), jnp.float32)
        _ctx_4096c = jax.random.dirichlet(jax.random.fold_in(_rk, 511), 0.3 * jnp.ones((16,), jnp.float32), (2, 512))
        _ctx_4096t = jnp.einsum('bsk,bkd->bsd', _ctx_4096c, _ctx_4096P)
        _ctx_4096t = _ctx_4096t * jax.lax.rsqrt(jnp.mean(jnp.square(_ctx_4096t)) + 1e-12) * 0.953939
        ctx_4096 = -5.72187e-05 + 0.999849 * (_ctx_4096t + 0.3 * jax.random.normal(jax.random.fold_in(_rk, 611), (2, 512, 512), jnp.float32))
        return (x, ctx_4096)
    x, ctx_4096 = _rec_inputs()

    def _L0_xattn_setup():
        import jax, jax.numpy as jnp
        import numpy as np
        QMIN = 0.0
        QMAX = 255.0

        def fake_quant(x, scale, zp):
            s = scale.reshape(())
            z = zp.reshape(())
            q = jnp.clip(jnp.round(x / s + z), QMIN, QMAX)
            return (q - z) * s
        key = jax.random.key(seed)
        k1, k2 = jax.random.split(key)
        B, M, K, N = (4, 256, 512, 512)
        x1 = jax.random.normal(k1, (B, M, K), dtype=jnp.float32)
        x2 = jax.random.normal(k2, (B, K, N), dtype=jnp.float32)
        x1_scale = jnp.full((1,), 8.0 / 255.0, dtype=jnp.float32)
        x1_zp = jnp.full((1,), 128.0, dtype=jnp.float32)
        x2_scale = jnp.full((1,), 8.0 / 255.0, dtype=jnp.float32)
        x2_zp = jnp.full((1,), 128.0, dtype=jnp.float32)
        return {'x1': x1, 'x2': x2, 'x1_scale': x1_scale, 'x1_zp': x1_zp, 'x2_scale': x2_scale, 'x2_zp': x2_zp}
    _L0_xattn_all = _L0_xattn_setup()
    _L0_xattn_in = {k: v for k, v in _L0_xattn_all.items() if k in ('x1_scale', 'x1_zp', 'x2_scale', 'x2_zp')}
    del _L0_xattn_all

    def _L0_ffn_setup():
        import jax, jax.numpy as jnp
        import numpy as np
        BLOCK = 64
        NF4_CODE = jnp.array([-1.0, -0.6961928009986877, -0.5250730514526367, -0.39491748809814453, -0.28444138169288635, -0.18477343022823334, -0.09105003625154495, 0.0, 0.07958029955625534, 0.16093020141124725, 0.24611230194568634, 0.33791524171829224, 0.44070982933044434, 0.5626170039176941, 0.7229568362236023, 1.0], dtype=jnp.float32)

        def dequant_nf4(q, absmax, shape):
            w = NF4_CODE[q.reshape(-1)]
            w = w.reshape(-1, BLOCK) * absmax[:, None]
            return w.reshape(shape)
        key = jax.random.key(seed)
        ks = jax.random.split(key, 7)
        HD, M = (512, 1792)
        nblk = HD * M // BLOCK
        x = jax.random.normal(ks[0], (2, 256, HD), dtype=jnp.float32)
        gate_q = jax.random.randint(ks[1], (M, HD), 0, 16, dtype=jnp.int32)
        up_q = jax.random.randint(ks[2], (M, HD), 0, 16, dtype=jnp.int32)
        down_q = jax.random.randint(ks[3], (HD, M), 0, 16, dtype=jnp.int32)
        gate_absmax = jax.random.uniform(ks[4], (nblk,), dtype=jnp.float32) * 0.05
        up_absmax = jax.random.uniform(ks[5], (nblk,), dtype=jnp.float32) * 0.05
        down_absmax = jax.random.uniform(ks[6], (nblk,), dtype=jnp.float32) * 0.05
        return {'x': x, 'gate_q': gate_q, 'gate_absmax': gate_absmax, 'up_q': up_q, 'up_absmax': up_absmax, 'down_q': down_q, 'down_absmax': down_absmax}
    _L0_ffn_all = _L0_ffn_setup()
    _L0_ffn_in = {k: v for k, v in _L0_ffn_all.items() if k in ('gate_q', 'gate_absmax', 'up_q', 'up_absmax', 'down_q', 'down_absmax')}
    del _L0_ffn_all

    def _L1_xattn_setup():
        import jax, jax.numpy as jnp
        import numpy as np
        HEADS = 32
        KV_HEADS = 8
        HEAD_DIM = 128
        EPS = 1e-06

        def rms_norm(x, w):
            var = jnp.mean(jnp.square(x.astype(jnp.float32)), axis=-1, keepdims=True)
            return (x.astype(jnp.float32) * jax.lax.rsqrt(var + EPS)).astype(x.dtype) * w
        key = jax.random.key(seed)
        ks = jax.random.split(key, 6)
        bsz, n_lat, seq, hidden = (8, 64, 512, 512)
        return {'latents': jax.random.normal(ks[0], (bsz, n_lat, hidden), jnp.float32), 'context': jax.random.normal(ks[1], (bsz, seq, hidden), jnp.float32), 'Wq': jax.random.normal(ks[2], (hidden, HEADS * HEAD_DIM), jnp.float32) * 0.02, 'Wk': jax.random.normal(ks[3], (hidden, KV_HEADS * HEAD_DIM), jnp.float32) * 0.02, 'Wv': jax.random.normal(ks[4], (hidden, KV_HEADS * HEAD_DIM), jnp.float32) * 0.02, 'Wo': jax.random.normal(ks[5], (HEADS * HEAD_DIM, hidden), jnp.float32) * 0.02, 'q_norm_w': jnp.ones((HEAD_DIM,), jnp.float32), 'k_norm_w': jnp.ones((HEAD_DIM,), jnp.float32)}
    _L1_xattn_all = _L1_xattn_setup()
    _L1_xattn_in = {k: v for k, v in _L1_xattn_all.items() if k in ('Wq', 'Wk', 'Wv', 'Wo', 'q_norm_w', 'k_norm_w')}
    del _L1_xattn_all

    def _L1_ffn_setup():
        import jax, jax.numpy as jnp
        import numpy as np
        HIDDEN = 512
        MOE_INTER = 128
        SHARED_INTER = 512
        NUM_EXPERTS = 16
        TOP_K = 2

        def _moe_forward(x, gate_w, w_gate_up, w_down, shared_w_gate_up, shared_w_down):
            orig_shape = x.shape
            x2 = x.reshape(-1, orig_shape[-1])
            gu_s = x2 @ shared_w_gate_up.T
            g_s, u_s = jnp.split(gu_s, 2, axis=-1)
            shared_out = jax.nn.silu(g_s) * u_s @ shared_w_down.T
            logits = x2 @ gate_w.T
            probs = jax.nn.softmax(logits, axis=-1)
            topk_vals, topk_idx = jax.lax.top_k(probs, TOP_K)
            topk_vals = topk_vals / jnp.sum(topk_vals, axis=-1, keepdims=True)
            combine = jnp.sum(jax.nn.one_hot(topk_idx, NUM_EXPERTS, dtype=x2.dtype) * topk_vals[..., None], axis=1)
            gu = jnp.einsum('th,eih->eti', x2, w_gate_up)
            g, u = jnp.split(gu, 2, axis=-1)
            act = jax.nn.silu(g) * u
            out_e = jnp.einsum('eti,ehi->eth', act, w_down)
            moe_out = jnp.einsum('eth,te->th', out_e, combine)
            return (moe_out + shared_out).reshape(orig_shape)
        key = jax.random.key(seed)
        ks = jax.random.split(key, 6)
        s = 0.02
        hidden_states = jax.random.normal(ks[0], (2, 256, HIDDEN), dtype=jnp.float32)
        gate_w = jax.random.normal(ks[1], (NUM_EXPERTS, HIDDEN), dtype=jnp.float32) * s
        w_gate_up = jax.random.normal(ks[2], (NUM_EXPERTS, 2 * MOE_INTER, HIDDEN), dtype=jnp.float32) * s
        w_down = jax.random.normal(ks[3], (NUM_EXPERTS, HIDDEN, MOE_INTER), dtype=jnp.float32) * s
        shared_w_gate_up = jax.random.normal(ks[4], (2 * SHARED_INTER, HIDDEN), dtype=jnp.float32) * s
        shared_w_down = jax.random.normal(ks[5], (HIDDEN, SHARED_INTER), dtype=jnp.float32) * s
        return {'hidden_states': hidden_states, 'gate_w': gate_w, 'w_gate_up': w_gate_up, 'w_down': w_down, 'shared_w_gate_up': shared_w_gate_up, 'shared_w_down': shared_w_down}
    _L1_ffn_all = _L1_ffn_setup()
    _L1_ffn_in = {k: v for k, v in _L1_ffn_all.items() if k in ('gate_w', 'w_gate_up', 'w_down', 'shared_w_gate_up', 'shared_w_down')}
    del _L1_ffn_all
    return {'x': x, 'ctx_4096': ctx_4096, 'L0_xattn_x1_scale': _L0_xattn_in['x1_scale'], 'L0_xattn_x1_zp': _L0_xattn_in['x1_zp'], 'L0_xattn_x2_scale': _L0_xattn_in['x2_scale'], 'L0_xattn_x2_zp': _L0_xattn_in['x2_zp'], 'L0_ffn_gate_q': _L0_ffn_in['gate_q'], 'L0_ffn_gate_absmax': _L0_ffn_in['gate_absmax'], 'L0_ffn_up_q': _L0_ffn_in['up_q'], 'L0_ffn_up_absmax': _L0_ffn_in['up_absmax'], 'L0_ffn_down_q': _L0_ffn_in['down_q'], 'L0_ffn_down_absmax': _L0_ffn_in['down_absmax'], 'L1_xattn_Wq': _L1_xattn_in['Wq'], 'L1_xattn_Wk': _L1_xattn_in['Wk'], 'L1_xattn_Wv': _L1_xattn_in['Wv'], 'L1_xattn_Wo': _L1_xattn_in['Wo'], 'L1_xattn_q_norm_w': _L1_xattn_in['q_norm_w'], 'L1_xattn_k_norm_w': _L1_xattn_in['k_norm_w'], 'L1_ffn_gate_w': _L1_ffn_in['gate_w'], 'L1_ffn_w_gate_up': _L1_ffn_in['w_gate_up'], 'L1_ffn_w_down': _L1_ffn_in['w_down'], 'L1_ffn_shared_w_gate_up': _L1_ffn_in['shared_w_gate_up'], 'L1_ffn_shared_w_down': _L1_ffn_in['shared_w_down']}

def reference(x, ctx_4096, L0_xattn_x1_scale, L0_xattn_x1_zp, L0_xattn_x2_scale, L0_xattn_x2_zp, L0_ffn_gate_q, L0_ffn_gate_absmax, L0_ffn_up_q, L0_ffn_up_absmax, L0_ffn_down_q, L0_ffn_down_absmax, L1_xattn_Wq, L1_xattn_Wk, L1_xattn_Wv, L1_xattn_Wo, L1_xattn_q_norm_w, L1_xattn_k_norm_w, L1_ffn_gate_w, L1_ffn_w_gate_up, L1_ffn_w_down, L1_ffn_shared_w_gate_up, L1_ffn_shared_w_down):
    import jax
    import jax.numpy as jnp

    def _L0_xattn_ref(x1, x2, x1_scale, x1_zp, x2_scale, x2_zp):
        import jax, jax.numpy as jnp
        import numpy as np
        QMIN = 0.0
        QMAX = 255.0

        def fake_quant(x, scale, zp):
            s = scale.reshape(())
            z = zp.reshape(())
            q = jnp.clip(jnp.round(x / s + z), QMIN, QMAX)
            return (q - z) * s
        q1 = fake_quant(x1, x1_scale, x1_zp)
        q2 = fake_quant(x2, x2_scale, x2_zp)
        return jnp.matmul(q1, q2)

    def _L0_ffn_ref(x, gate_q, gate_absmax, up_q, up_absmax, down_q, down_absmax):
        import jax, jax.numpy as jnp
        import numpy as np
        BLOCK = 64
        NF4_CODE = jnp.array([-1.0, -0.6961928009986877, -0.5250730514526367, -0.39491748809814453, -0.28444138169288635, -0.18477343022823334, -0.09105003625154495, 0.0, 0.07958029955625534, 0.16093020141124725, 0.24611230194568634, 0.33791524171829224, 0.44070982933044434, 0.5626170039176941, 0.7229568362236023, 1.0], dtype=jnp.float32)

        def dequant_nf4(q, absmax, shape):
            w = NF4_CODE[q.reshape(-1)]
            w = w.reshape(-1, BLOCK) * absmax[:, None]
            return w.reshape(shape)
        HD = x.shape[-1]
        M = gate_q.shape[0]
        Wg = dequant_nf4(gate_q, gate_absmax, (M, HD))
        Wu = dequant_nf4(up_q, up_absmax, (M, HD))
        Wd = dequant_nf4(down_q, down_absmax, (HD, M))
        g = jnp.einsum('bsh,mh->bsm', x, Wg)
        u = jnp.einsum('bsh,mh->bsm', x, Wu)
        h = jax.nn.silu(g) * u
        return jnp.einsum('bsm,hm->bsh', h, Wd)

    def _L1_xattn_ref(latents, context, Wq, Wk, Wv, Wo, q_norm_w, k_norm_w):
        import jax, jax.numpy as jnp
        import numpy as np
        HEADS = 32
        KV_HEADS = 8
        HEAD_DIM = 128
        EPS = 1e-06

        def rms_norm(x, w):
            var = jnp.mean(jnp.square(x.astype(jnp.float32)), axis=-1, keepdims=True)
            return (x.astype(jnp.float32) * jax.lax.rsqrt(var + EPS)).astype(x.dtype) * w
        bsz, q_len, hidden = latents.shape
        kv = jnp.concatenate([context, latents], axis=1)
        kv_len = kv.shape[1]
        groups = HEADS // KV_HEADS
        q = (latents @ Wq).reshape(bsz, q_len, HEADS, HEAD_DIM).transpose(0, 2, 1, 3)
        k = (kv @ Wk).reshape(bsz, kv_len, KV_HEADS, HEAD_DIM).transpose(0, 2, 1, 3)
        v = (kv @ Wv).reshape(bsz, kv_len, KV_HEADS, HEAD_DIM).transpose(0, 2, 1, 3)
        q = rms_norm(q, q_norm_w)
        k = rms_norm(k, k_norm_w)
        qg = q.reshape(bsz, KV_HEADS, groups, q_len, HEAD_DIM)
        scale = 1.0 / np.sqrt(HEAD_DIM)
        scores = jnp.einsum('bhgqd,bhkd->bhgqk', qg, k) * scale
        probs = jax.nn.softmax(scores.astype(jnp.float32), axis=-1).astype(q.dtype)
        out = jnp.einsum('bhgqk,bhkd->bhgqd', probs, v)
        out = out.reshape(bsz, HEADS, q_len, HEAD_DIM).transpose(0, 2, 1, 3)
        out = out.reshape(bsz, q_len, HEADS * HEAD_DIM)
        return out @ Wo

    def _L1_ffn_ref(hidden_states, gate_w, w_gate_up, w_down, shared_w_gate_up, shared_w_down):
        import jax, jax.numpy as jnp
        import numpy as np
        HIDDEN = 512
        MOE_INTER = 128
        SHARED_INTER = 512
        NUM_EXPERTS = 16
        TOP_K = 2

        def _moe_forward(x, gate_w, w_gate_up, w_down, shared_w_gate_up, shared_w_down):
            orig_shape = x.shape
            x2 = x.reshape(-1, orig_shape[-1])
            gu_s = x2 @ shared_w_gate_up.T
            g_s, u_s = jnp.split(gu_s, 2, axis=-1)
            shared_out = jax.nn.silu(g_s) * u_s @ shared_w_down.T
            logits = x2 @ gate_w.T
            probs = jax.nn.softmax(logits, axis=-1)
            topk_vals, topk_idx = jax.lax.top_k(probs, TOP_K)
            topk_vals = topk_vals / jnp.sum(topk_vals, axis=-1, keepdims=True)
            combine = jnp.sum(jax.nn.one_hot(topk_idx, NUM_EXPERTS, dtype=x2.dtype) * topk_vals[..., None], axis=1)
            gu = jnp.einsum('th,eih->eti', x2, w_gate_up)
            g, u = jnp.split(gu, 2, axis=-1)
            act = jax.nn.silu(g) * u
            out_e = jnp.einsum('eti,ehi->eth', act, w_down)
            moe_out = jnp.einsum('eth,te->th', out_e, combine)
            return (moe_out + shared_out).reshape(orig_shape)
        return _moe_forward(hidden_states, gate_w, w_gate_up, w_down, shared_w_gate_up, shared_w_down)
    x = x + _L0_xattn_ref(_layernorm(x, axis=-1), ctx_4096, L0_xattn_x1_scale, L0_xattn_x1_zp, L0_xattn_x2_scale, L0_xattn_x2_zp)
    x = x + _L0_ffn_ref(_layernorm(x, axis=-1), L0_ffn_gate_q, L0_ffn_gate_absmax, L0_ffn_up_q, L0_ffn_up_absmax, L0_ffn_down_q, L0_ffn_down_absmax)
    x = x + _L1_xattn_ref(_layernorm(x, axis=-1), ctx_4096, L1_xattn_Wq, L1_xattn_Wk, L1_xattn_Wv, L1_xattn_Wo, L1_xattn_q_norm_w, L1_xattn_k_norm_w)
    x = x + _L1_ffn_ref(_layernorm(x, axis=-1), L1_ffn_gate_w, L1_ffn_w_gate_up, L1_ffn_w_down, L1_ffn_shared_w_gate_up, L1_ffn_shared_w_down)
    return x

_drawn_inputs = setup_inputs


def setup_inputs(seed=0):
    import zlib

    import numpy as np

    out = dict(_drawn_inputs(seed))
    spreads = {'L1_xattn_q_norm_w': (1.0, 0.6), 'L1_xattn_k_norm_w': (1.0, 0.6)}
    factors = {'L0_ffn_gate_absmax': 8.0,
     'L0_ffn_up_absmax': 8.0,
     'L0_ffn_down_absmax': 8.0,
     'L1_xattn_Wq': 8.0,
     'L1_xattn_Wk': 8.0,
     'L1_xattn_Wv': 5.033,
     'L1_xattn_Wo': 5.102,
     'L1_ffn_gate_w': 8.0,
     'L1_ffn_w_gate_up': 8.0,
     'L1_ffn_w_down': 8.0,
     'L1_ffn_shared_w_gate_up': 8.0,
     'L1_ffn_shared_w_down': 8.0}
    for name, (base, spread) in spreads.items():
        noise = np.random.default_rng([zlib.crc32(name.encode()), seed]).standard_normal(out[name].shape)
        drawn = base * np.exp(spread * noise) if base else spread * noise
        out[name] = jnp.asarray(drawn.astype(out[name].dtype))
    for name, factor in factors.items():
        out[name] = (out[name] * factor).astype(out[name].dtype)
    return out
```

```python
import concourse.bass as bass
from concourse import mybir
from contextlib import ExitStack

P = 128
TOK, D, NB = 512, 512, 2
CTX = 512
TT, KD = TOK // P, D // P
CT = NB * CTX // P
FF = 1792
UNITS = FF // P
HEADS, KVH, HD = 32, 8, 128
GROUP = HEADS // KVH
KEYS = CTX + TOK // NB
KB = KEYS // P
EXPERTS, SHARED, INTER = 16, 4, 128
NE = EXPERTS + SHARED
WSCALE = 64.0
INV = 1.0 / WSCALE
LN_EPS, RMS_EPS = 1e-5, 1e-6
ROUND = 12582912.0
RSQRT_SEED = 1597463007.0

NF4_LEAD = 0.003969766543852396
NF4_FACTORS = [
    (-0.035814158618450165, 0.01144565548747778), (-3.722414255142212, 0.013174708932638168),
    (-0.4697154760360718, 0.1573619842529297), (-3.2984719276428223, 0.1701432317495346),
    (-1.0957497358322144, 0.33853575587272644), (-2.6926143169403076, 0.37515297532081604),
    (-1.9447404146194458, 0.3761288523674011)]
NF = len(NF4_FACTORS)
UNIT = 3 * D
HALF = UNIT // 2
ITER = UNITS // 2


class Steps:

    def __init__(self, eng, sem):
        self.eng, self.sem, self.base, self.k = eng, sem, 0, 0

    def did(self, instruction):
        instruction.then_inc(self.sem, 1)
        self.k += 1
        return self.base + self.k

    def wait(self, value=None):
        self.eng.wait_ge(self.sem, self.base + self.k if value is None else value)

    def at(self, base):
        self.base, self.k = base, 0


def wait_past(eng, sem, value):
    if not isinstance(value, int) or value > 0:
        eng.wait_ge(sem, value)


def bass_xattn_ffn_two_layers(nc, x, ctx, ctx_t, quant, codes, absmax, wk, wv, wq, wo, norms,
                              router_w, experts, iota, out):
    f32, f16, bf16 = mybir.dt.float32, mybir.dt.float16, mybir.dt.bfloat16
    i32, u32 = mybir.dt.int32, mybir.dt.uint32
    ALU, ACT, AX = mybir.AluOpType, mybir.ActivationFunctionType, mybir.AxisListType.X

    ctxs = ExitStack()
    with ctxs:
        arena = ctxs.enter_context(nc.sbuf_tensor("arena", [P, 204 * 256], f32))

        def place(kib, shape, dtype=f32):
            n = 1
            for s in shape:
                n *= s
            words = n if dtype in (f32, i32) else n // 2
            start = int(kib * 256)
            v = arena[:, start:start + words]
            if dtype is not f32:
                v = v.bitcast(dtype)
            if len(shape) == 2:
                v = v.rearrange("p (a b) -> p a b", a=shape[0])
            if len(shape) == 3:
                v = v.rearrange("p (a b c) -> p a b c", a=shape[0], b=shape[1])
            return v

        x_res = place(0, (TT, D))
        xn = place(112, (TT, D))
        xnT32 = place(120, (KD, TOK))
        xnT = [place(120, (KD, TOK), f16), place(124, (KD, TOK), f16)]
        KTc = [place(8, (KVH, NB * CTX), f16), place(24, (KVH, NB * CTX), f16)]
        Vc = [place(40, (CT, KVH * HD), f16), place(56, (CT, KVH * HD), f16)]
        KTl = [place(128, (KVH, TOK), f16), place(136, (KVH, TOK), f16)]
        Vl = [place(144, (TT, KVH * HD), f16), place(152, (TT, KVH * HD), f16)]
        w_k = [place(72, (KD, KVH * HD), f16), place(80, (KD, KVH * HD), f16)]
        w_v = [place(88, (KD, KVH * HD), f16), place(96, (KD, KVH * HD), f16)]
        k_raw = place(104, (KVH, HD))
        k_sq = place(108, (KVH, HD))
        ctx32 = place(8, (CT, D))
        ctxT32 = place(40, (KD, NB * CTX))
        wk32 = place(24, (KD, KVH * HD))
        wv32 = place(56, (KD, KVH * HD))
        ctxT = [place(128, (KD, NB * CTX), f16), place(136, (KD, NB * CTX), f16)]
        ctx_q = place(104, (CT, D), bf16)
        x_q = place(144, (TT, D), bf16)
        x_qT = place(156, (KD, TOK), bf16)
        h0 = [place(144, (TOK,)), place(146, (TOK,))]
        w0 = [place(148, (UNIT,)), place(154, (UNIT,))]
        code_buf = [place(160, (UNIT,), i32), place(166, (UNIT,), i32)]
        absmax_buf = [place(172, (UNIT,)), place(178, (UNIT,))]
        square_buf = [place(184, (UNIT,)), place(190, (UNIT,))]
        gate_act = place(196, (TOK,))
        shifted = place(198, (UNIT,))
        PT = [[place(72 + 12 * b + 6 * v, (KB, GROUP * P), f16) for v in range(2)] for b in range(2)]
        probs = [place(96 + 3 * b, (KEYS,)) for b in range(4)]
        OT = [[place(108 + 2 * b + v, (GROUP, P), f16) for v in range(2)] for b in range(2)]
        wo32 = place(112, (GROUP, D))
        QT = place(160, (2, 2, GROUP * TOK), f16)
        wq32 = place(176, (KD, GROUP * HD))
        w_q = [place(184, (KD, GROUP * HD), f16), place(188, (KD, GROUP * HD), f16)]
        w_o = [place(192, (GROUP, D), f16), place(196, (GROUP, D), f16)]
        q_sq = place(200, (2, TOK))
        EW = 3 * D
        ew32 = [place(k, (EW,)) for k in (176, 182, 8, 14)]
        e_w = [[place(k, (EW,), f16), place(m, (EW,), f16)] for k, m in ((160, 163), (188, 200), (20, 23), (26, 29))]
        e_gate = [place(50 + 2 * b, (TOK,)) for b in range(2)]
        e_h = [place(54 + 2 * b, (TOK,)) for b in range(2)]
        e_hT = [[place(58 + 2 * b + v, (TOK,), f16) for v in range(2)] for b in range(2)]

        def small(name, shape, dtype=f32):
            return ctxs.enter_context(nc.sbuf_tensor(name, shape, dtype))

        ident = small("ident", [P, P])
        ident16 = small("ident16", [P, P], bf16)
        ones16 = small("ones16", [P, P], bf16)
        ones = small("ones", [P, 1])
        factor_b = small("factor_b", [P, NF])
        turn = small("turn", [P, 2])
        quant_in = small("quant_in", [P, 4])
        qp = small("qp", [P, 8])
        rowsum = small("rowsum", [P, TT])
        row_term = small("row_term", [P, TT])
        norm_in = small("norm_in", [P, 2])
        w_qk = small("w_qk", [P, 1])
        bn = small("bn", [P, TT, 6])
        mv = small("mv", [P, TT, 2])
        ln_r = small("ln_r", [P, TT])
        ln_v = small("ln_v", [P, TT])
        ln_t = small("ln_t", [P, TT])
        k_ss = small("k_ss", [P, KVH])
        k_r = small("k_r", [P, KVH])
        k_v = small("k_v", [P, KVH])
        k_t = small("k_t", [P, KVH])
        rq_next = small("rq_next", [P, GROUP * TT])
        rq_v = small("rq_v", [P, GROUP * TT])
        rq_t = small("rq_t", [P, GROUP * TT])
        rq_now = small("rq_now", [P, GROUP * TT])
        row_max = small("row_max", [P, 4])
        neg_max = small("neg_max", [P, 4])
        row_sum = small("row_sum", [P, 4])
        inv_sum = small("inv_sum", [P, 4])
        rw32 = small("rw32", [P, KD, EXPERTS])
        r_w = [small("r_w_hi", [P, KD, EXPERTS], f16), small("r_w_lo", [P, KD, EXPERTS], f16)]
        iota_in = small("iota_in", [P, EXPERTS])
        logits = place(62, (TT, EXPERTS))
        rprob = place(62.25, (TT, EXPERTS))
        r_max = small("r_max", [P, TT])
        r_neg = small("r_neg", [P, TT])
        r_sum = small("r_sum", [P, TT])
        r_inv = small("r_inv", [P, TT])
        top8 = small("top8", [P, TT, 8])
        top8i = small("top8i", [P, TT, 8], u32)
        top_i = small("top_i", [P, TT, 2])
        top_w = small("top_w", [P, TT, 2])
        pick = place(62.5, (TT, 2, EXPERTS))
        combine = small("combine", [P, TT, NE])

        psum = ctxs.enter_context(nc.psum_tensor("psum", [P, 8 * 512], f32))
        bank = [psum[:, b * 512:(b + 1) * 512] for b in range(8)]
        DOWN, GATE, UP, KV0, KV1 = bank[0:4], bank[4], bank[5], bank[6], bank[7]
        SCORE = [psum[:, 0:KEYS], psum[:, 1024:1024 + KEYS]]
        PT_BANK = bank[4:6]
        O_BANK, PROJ = bank[6], bank[7]
        SUMSQ = PT_BANK[0][:, 3 * P:3 * P + GROUP * TT]
        LN_BANK0, LN_BANK1, LN_BANK2 = bank[0:4], (bank[2], bank[3], bank[4], bank[5]), bank[4:8]
        Q0_BANK = (bank[7], bank[2], bank[3], bank[6])

        def sem(name):
            return ctxs.enter_context(nc.semaphore(name))

        quant_loaded, norms_loaded, x_loaded = map(sem, ("quant_loaded", "norms_loaded", "x_loaded"))
        ctx_loaded = [sem("ctx_loaded0"), sem("ctx_loaded1")]
        ctxT_loaded, wk_loaded, wv_loaded, router_loaded = map(sem, ("ctxT_loaded", "wk_loaded", "wv_loaded", "router_loaded"))
        codes_loaded = [sem("codes_loaded0"), sem("codes_loaded1")]
        absmax_loaded = [sem("absmax_loaded0"), sem("absmax_loaded1")]
        wq_loaded, wo_loaded = sem("wq_loaded"), sem("wo_loaded")
        expert_loaded = [sem(f"expert_loaded{b}") for b in range(4)]
        stored = sem("stored")
        dve_step, pool_step, act_step = sem("dve_step"), sem("pool_step"), sem("act_step")
        consts_ready, quant_ready, x_normed, x_affine, ctx_affine = map(sem, ("consts_ready", "quant_ready", "x_normed", "x_affine", "ctx_affine"))
        x_quantised, ctx_quantised, x_qT_psum, x_qT_ready = map(sem, ("x_quantised", "ctx_quantised", "x_qT_psum", "x_qT_ready"))
        colsum_done, qprod_done = sem("colsum_done"), sem("qprod_done")
        ctxT_hi, ctxT_split, wk_hi, wk_split, wv_hi, wv_split = map(sem, ("ctxT_hi", "ctxT_split", "wk_hi", "wk_split", "wv_hi", "wv_split"))
        ln_transposed, ln_hi, ln_ready, ln_rstd_ready, w_qk_ready = map(sem, ("ln_transposed", "ln_hi", "ln_ready", "ln_rstd_ready", "w_qk_ready"))
        turn_set = sem("turn_set")
        codes_shifted, codes_scaled, squares_ready, factors_applied = map(sem, ("codes_shifted", "codes_scaled", "squares_ready", "factors_applied"))
        gate_done, up_done, gate_activated, h_ready, down_done = map(sem, ("gate_done", "up_done", "gate_activated", "h_ready", "down_done"))
        ffn_added = sem("ffn_added")
        k_projected, k_copied, k_squared, k_rstd, k_normed = map(sem, ("k_projected", "k_copied", "k_squared", "k_rstd", "k_normed"))
        k_transposed, k_hi, k_split, v_projected, v_hi, v_split = map(sem, ("k_transposed", "k_hi", "k_split", "v_projected", "v_hi", "v_split"))
        wq_hi, wq_split, wo_hi, wo_split = map(sem, ("wq_hi", "wq_split", "wo_hi", "wo_split"))
        q_projected, q_hi, q_squared, q_split, q_sumsq, sumsq_read, rq_ready = map(sem, ("q_projected", "q_hi", "q_squared", "q_split", "q_sumsq", "sumsq_read", "rq_ready"))
        scores_ready, neg_max_ready, probs_ready, sum_inverted, probs_normed = map(sem, ("scores_ready", "neg_max_ready", "probs_ready", "sum_inverted", "probs_normed"))
        probs_transposed, PT_hi, PT_split = sem("probs_transposed"), sem("PT_hi"), sem("PT_split")
        o_done, o_hi, o_split, o_projected, attn_added = map(sem, ("o_done", "o_hi", "o_split", "o_projected", "attn_added"))
        logits_done, logits_read, router_shifted, router_exp, combine_ready = map(sem, ("logits_done", "logits_read", "router_shifted", "router_exp", "combine_ready"))
        ew_hi, ew_split, e_gate_done, e_up_done, e_gate_act = map(sem, ("ew_hi", "ew_split", "e_gate_done", "e_up_done", "e_gate_act"))
        e_h_ready, e_h_hi, e_h_split, e_down_done, moe_added = map(sem, ("e_h_ready", "e_h_hi", "e_h_split", "e_down_done", "moe_added"))

        block = ctxs.enter_context(nc.Block())

        PARTS = ((0, 0), (0, 1), (1, 0))
        STEPS = GROUP * TT

        VALUES_0, VALUES_1, OUT, WO, ADD = 7, 9, 10, 12, 13
        LAG = 2

        def due(g, n, delay, first=False, last=False):
            if (n - delay) % GROUP or (first and n < delay) or (last and n >= delay):
                return None
            return g * TT + (n - delay) // GROUP

        def flat(v):
            return v.rearrange("p a b -> p (a b)")

        def ctx_values(part, z):
            return lambda h: Vc[part][:, bass.ds(z, 1), h * 512:(h + 1) * 512].rearrange("p a n -> p (a n)")

        def own_values(part, t):
            return lambda h: Vl[part][:, t, h * 512:(h + 1) * 512]

        def ctx_keys(part, z):
            return lambda h: KTc[part][:, 4 * h:4 * h + 4, bass.ds(z * P, P)]

        def own_keys(part, t):
            return lambda h: KTl[part][:, 4 * h:4 * h + 4, t * P:(t + 1) * P]

        def queries(g, part, h, s=None):
            start, size = (h * TOK, TOK) if s is None else (h * TOK + s * P, P)
            return QT[:, bass.ds(g % 2, 1), part, start:start + size].rearrange("p a n -> p (a n)")

        def PT_slot(part, n, c):
            return PT[(n // GROUP) % 2][part][:, 3 * c:3 * c + 3, (n % GROUP) * P:(n % GROUP + 1) * P]

        def loaded_after(e, b):
            return (e - b) * 4 + 16

        @block.sync
        def _(sp):
            def load_unit(i, b):
                u = 2 * i + b
                wait_past(sp, squares_ready, NF * (u - 1))
                row = bass.ds(u, 1)
                sp.dma_start(code_buf[b], codes[row, :, :].rearrange("a p n -> p (a n)")).then_inc(codes_loaded[b], 16)
                sp.dma_start(absmax_buf[b], absmax[row, :, :].rearrange("a h n -> h a n").to_broadcast((2, P // 2, UNIT)))\
                    .then_inc(absmax_loaded[b], 16)

            sp.dma_start(x_res, x.rearrange("(t p) n -> p t n", p=P)).then_inc(x_loaded, 16)
            for c in range(4):
                sp.dma_start(quant_in[:, c:c + 1], quant[c:c + 1, :].to_broadcast((P, 1))).then_inc(quant_loaded, 16)
            for b in range(NB):
                sp.dma_start(ctx32[:, b * KD:(b + 1) * KD, :], ctx[b * CTX:(b + 1) * CTX, :].rearrange("(t p) n -> p t n", p=P))\
                    .then_inc(ctx_loaded[b], 16)
            load_unit(0, 0)
            sp.dma_start(ctxT32, ctx_t.rearrange("(k p) n -> p k n", p=P)).then_inc(ctxT_loaded, 16)
            sp.dma_start(wv32, wv.rearrange("(k p) n -> p k n", p=P)).then_inc(wv_loaded, 16)
            sp.dma_start(wk32, wk.rearrange("(k p) n -> p k n", p=P)).then_inc(wk_loaded, 16)
            sp.dma_start(norm_in[:, :], norms).then_inc(norms_loaded, 16)
            sp.dma_start(rw32[:, :, :], router_w.rearrange("(k p) e -> p k e", p=P)).then_inc(router_loaded, 16)
            sp.dma_start(iota_in[:, :], iota).then_inc(router_loaded, 16)

            load_unit(0, 1)
            with sp.Fori(1, ITER) as i:
                for b in range(2):
                    load_unit(i, b)

            def load_wq(g):
                wait_past(sp, wq_split, g)
                sp.dma_start(wq32, wq[:, bass.ds(g * (GROUP * HD), GROUP * HD)].rearrange("(k p) n -> p k n", p=P)).then_inc(wq_loaded, 16)

            def load_wo(g):
                wait_past(sp, wo_split, g)
                sp.dma_start(wo32, wo[bass.ds(g * (GROUP * HD), GROUP * HD), :].rearrange("(h p) n -> p h n", p=P)).then_inc(wo_loaded, 16)

            sp.wait_ge(factors_applied, 2 * NF * UNITS)
            load_wq(0)
            load_wq(1)
            sp.wait_ge(ln_transposed, 2 * KD)
            load_wo(0)
            load_wq(2)
            with sp.Fori(1, KVH - 2) as g:
                load_wo(g)
                load_wq(g + 2)
            load_wo(KVH - 2)
            load_wo(KVH - 1)
            sp.wait_ge(q_projected, KVH * GROUP)

            def load_expert(e, b):
                wait_past(sp, ew_split, e - 3)
                sp.dma_start(ew32[b], experts[bass.ds(e, 1), :, :].rearrange("a p n -> p (a n)")).then_inc(expert_loaded[b], 16)

            load_expert(0, 0)
            load_expert(1, 1)
            sp.wait_ge(scores_ready, KVH * GROUP * TT)
            load_expert(2, 2)
            load_expert(3, 3)
            with sp.Fori(1, NE // 4) as i:
                for b in range(4):
                    load_expert(4 * i + b, b)
            for t in range(TT):
                sp.wait_ge(moe_added, TT * (NE - 1) + t + 1)
                sp.dma_start(out[t * P:(t + 1) * P, :], x_res[:, t, :]).then_inc(stored, 16)
            sp.wait_ge(stored, 16 * TT)

        @block.gpsimd
        def _(pool):
            step = Steps(pool, pool_step)
            for m in (ident, ident16):
                step.did(pool.memset(m[:, :], 0.0))
            pool.memset(ones16[:, :], 1.0).then_inc(consts_ready, 1)
            pool.memset(ones[:, :], 1.0).then_inc(consts_ready, 1)
            pool.memset(combine[:, :, 0:SHARED], INV).then_inc(consts_ready, 1)
            for f, (b, _) in enumerate(NF4_FACTORS):
                pool.memset(factor_b[:, f:f + 1], b).then_inc(consts_ready, 1)
            step.wait()
            for m in (ident, ident16):
                pool.affine_select(out=m[:, :], in_=m[:, :], compare_op=ALU.not_equal, fill=1.0, base=0,
                                   pattern=[[-1, P]], channel_multiplier=1).then_inc(consts_ready, 1)
            pool.memset(turn[:, 1:2], 0.0).then_inc(turn_set, 1)
            pool.wait_ge(turn_set, 1)

            def scale_codes(i, b):
                u = 2 * i + b
                wait_past(pool, codes_scaled, u)
                pool.wait_ge(codes_loaded[b], 16 * (i + 1))
                pool.tensor_tensor(turn[:, 0:1], turn[:, 1:2], turn[:, 1:2], ALU.mult)
                pool.tensor_scalar(shifted, code_buf[b], -7.0, 1.0, ALU.add, ALU.mult).then_inc(codes_shifted, 1)
                pool.wait_ge(codes_shifted, u + 1)
                pool.wait_ge(absmax_loaded[b], 16 * (i + 1))
                pool.tensor_tensor(absmax_buf[b], shifted, absmax_buf[b], ALU.mult).then_inc(codes_scaled, 1)

            scale_codes(0, 0)
            for k in range(KD):
                pool.wait_ge(ctxT_hi, k + 1)
                pool.tensor_tensor(ctxT[1][:, k, :], ctxT32[:, k, :], ctxT[0][:, k, :], ALU.subtract).then_inc(ctxT_split, 1)
            def split_weights(ks, w32, parts, hi, split):
                for k in ks:
                    pool.wait_ge(hi, k + 1)
                    n = step.did(pool.tensor_scalar(w32[:, k, :], w32[:, k, :], WSCALE, 1.0, ALU.mult, ALU.mult))
                    step.wait(n)
                    pool.tensor_tensor(parts[1][:, k, :], w32[:, k, :], parts[0][:, k, :], ALU.subtract).then_inc(split, 1)

            split_weights(range(KD), wv32, w_v, wv_hi, wv_split)

            def norm_keys(z):
                pool.wait_ge(k_rstd, z + 1)
                pool.tensor_tensor(k_raw, k_raw, k_r[:, :, None].to_broadcast((P, KVH, HD)), ALU.mult).then_inc(k_normed, 1)

            scale_codes(0, 1)
            split_weights(range(2), wk32, w_k, wk_hi, wk_split)
            scale_codes(1, 0)
            split_weights(range(2, KD), wk32, w_k, wk_hi, wk_split)
            scale_codes(1, 1)
            with pool.Fori(1, ITER - 1) as i:
                scale_codes(i + 1, 0)
                norm_keys(i - 1)
                scale_codes(i + 1, 1)
            with pool.Fori(ITER - 2, CT + TT) as z:
                norm_keys(z)

            with pool.Fori(0, KVH) as g:
                for n in range(STEPS):
                    pool.wait_ge(sum_inverted, g * STEPS + n + 1)
                    pool.tensor_tensor(probs[n % 4], probs[n % 4], inv_sum[:, n % 4:n % 4 + 1].to_broadcast((P, KEYS)), ALU.mult)\
                        .then_inc(probs_normed, 1)

        @block.scalar
        def _(act):
            def copy(o, i, scale, done):
                nc.scalar.activation(o, i, ACT.Copy, scale=scale).then_inc(done, 1)

            act.wait_ge(quant_ready, 1)
            def ctx_to_quants(b):
                act.wait_ge(ctx_loaded[b], 16)
                v = ctx32[:, b * KD:(b + 1) * KD, :]
                nc.scalar.activation(v, v, ACT.Identity, scale=qp[:, 1:2], bias=quant_in[:, 3:4]).then_inc(ctx_affine, 1)

            ctx_to_quants(0)
            for t in range(TT):
                act.wait_ge(x_normed, t + 1)
                nc.scalar.activation(xn[:, t, :], xn[:, t, :], ACT.Identity, scale=qp[:, 0:1], bias=quant_in[:, 1:2]).then_inc(x_affine, 1)
            ctx_to_quants(1)

            def squares(i, b, factors):
                u = 2 * i + b
                for f in factors:
                    if f == 0:
                        act.wait_ge(codes_loaded[b], 16 * (i + 1))
                    wait_past(act, factors_applied, 2 * (NF * u + f - 1))
                    nc.scalar.activation(square_buf[(NF * b + f) % 2], code_buf[b], ACT.Square, scale=0.25,
                                         bias=factor_b[:, f:f + 1]).then_inc(squares_ready, 1)

            def activate_gate(u):
                act.wait_ge(gate_done, u + 1)
                nc.scalar.activation(gate_act, GATE, ACT.Silu, scale=NF4_LEAD).then_inc(gate_activated, 1)

            def values_hi(z, dst, banks):
                for h in range(2):
                    act.wait_ge(v_projected, 2 * z + h + 1)
                    copy(dst(h), banks[h], INV, v_hi)

            def copy_keys(z):
                for h in range(2):
                    act.wait_ge(k_projected, 2 * z + h + 1)
                    wait_past(act, k_transposed, 2 * z)
                    copy(k_raw[:, 4 * h:4 * h + 4, :], (KV0, KV1)[h].rearrange("p (a b) -> p a b", a=4), INV, k_copied)
                act.wait_ge(k_copied, 2 * z + 2)
                nc.scalar.activation(k_sq, k_raw, ACT.Square).then_inc(k_squared, 1)

            def keys_hi(z, dst, banks):
                for h in range(2):
                    act.wait_ge(k_transposed, 2 * z + h + 1)
                    nc.scalar.activation(dst(h), banks[h].rearrange("p (a b) -> p a b", a=4), ACT.Copy,
                                         scale=w_qk[:, 0:1]).then_inc(k_hi, 1)

            def pair(i):
                n = i if isinstance(i, int) else 2
                if n > 0:
                    squares(i, 0, range(0, 2))
                    values_hi(i - 1, ctx_values(0, i - 1), (KV0, KV1))
                    squares(i, 0, range(2, 4))
                    activate_gate(2 * i - 1)
                    squares(i, 0, range(4, 5))
                if n > 1:
                    keys_hi(i - 2, ctx_keys(0, i - 2), (KV0, KV1))
                if n > 0:
                    squares(i, 0, range(5, NF))
                squares(i, 1, range(0, 3))
                if n > 0:
                    copy_keys(i - 1)
                squares(i, 1, range(3, 4))
                activate_gate(2 * i)
                squares(i, 1, range(4, NF))

            act.wait_ge(consts_ready, 3 + NF)
            squares(0, 0, range(0, 1))
            for k in range(KD):
                act.wait_ge(x_qT_psum, k + 1)
                copy(x_qT[:, k, :], bank[4 + k][:, 0:TOK // 2].bitcast(bf16), 1.0, x_qT_ready)
            squares(0, 0, range(1, 2))
            act.wait_ge(ctxT_loaded, 16)
            for k in range(KD):
                copy(ctxT[0][:, k, :], ctxT32[:, k, :], 1.0, ctxT_hi)
            squares(0, 0, range(2, 3))
            act.wait_ge(wv_loaded, 16)
            for k in range(KD):
                copy(w_v[0][:, k, :], wv32[:, k, :], WSCALE, wv_hi)
            act.wait_ge(wk_loaded, 16)
            for k in range(KD):
                copy(w_k[0][:, k, :], wk32[:, k, :], WSCALE, wk_hi)
            squares(0, 0, range(3, 4))
            for k in range(0, KD, 2):
                act.wait_ge(ln_transposed, k + 1)
                copy(xnT32[:, k, :], LN_BANK0[k], 1.0, ln_hi)
            squares(0, 0, range(4, NF))
            pair(0)
            pair(1)
            with act.Fori(2, ITER) as i:
                pair(i)
            z = ITER - 1
            values_hi(z, ctx_values(0, z), (KV0, KV1))
            activate_gate(UNITS - 1)
            keys_hi(z - 1, ctx_keys(0, z - 1), (KV0, KV1))
            copy_keys(z)
            values_hi(z + 1, ctx_values(0, z + 1), (GATE, UP))
            for k in range(KD):
                act.wait_ge(ln_transposed, KD + k + 1)
                copy(xnT[0][:, k, :], LN_BANK1[k], 1.0, ln_hi)
            keys_hi(z, ctx_keys(0, z), (bank[0], bank[1]))
            copy_keys(z + 1)

            def wq_part(g):
                act.wait_ge(wq_loaded, 16 * (g + 1))
                wait_past(act, q_projected, GROUP * g)
                copy(w_q[0], wq32, WSCALE, wq_hi)

            wq_part(0)
            for t in range(TT):
                z = CT + t
                values_hi(z, own_values(0, t), (GATE, UP))
                keys_hi(z - 1, own_keys(0, t - 1) if t else ctx_keys(0, z - 1), (bank[0], bank[1]))
                copy_keys(z)
            keys_hi(z, own_keys(0, TT - 1), (bank[0], bank[1]))

            def query_out(g, h, src):
                act.wait_ge(q_projected, GROUP * g + h + 1)
                copy(queries(g, 0, h), src, INV, q_hi)
                wait_past(act, q_sumsq, 2 * g + h // 2)
                nc.scalar.activation(q_sq[:, h % 2, :], src, ACT.Square, scale=INV).then_inc(q_squared, 1)

            for h in range(GROUP):
                query_out(0, h, Q0_BANK[h])
            wq_part(1)

            def transposed_hi(N, n):
                for c in range(2):
                    act.wait_ge(probs_transposed, 2 * N + c + 1)
                    copy(PT_slot(0, n, c), PT_BANK[c][:, 0:3 * P].rearrange("p (a b) -> p a b", a=3), 1.0, PT_hi)

            def out_hi(S, s):
                act.wait_ge(o_done, S + 1)
                copy(OT[s % 2][0], O_BANK.rearrange("p (a b) -> p a b", a=GROUP), 1.0, o_hi)

            def expert_hi(e, b):
                act.wait_ge(expert_loaded[b], loaded_after(e, b))
                copy(e_w[b][0], ew32[b], WSCALE, ew_hi)

            def attention(g, first=False, has_q=True, has_wq=True):
                for n in range(STEPS):
                    N = g * STEPS + n
                    S = due(g, n, OUT, first)
                    if S is not None:
                        out_hi(S, (n - OUT) // GROUP)
                    if n % GROUP == 3 and has_q:
                        query_out(g + 1, n // GROUP, PROJ)
                    if not first or n >= LAG:
                        transposed_hi(N - LAG, (n - LAG) % STEPS)
                    act.wait_ge(neg_max_ready, N + 1)
                    if not first or n >= 4:
                        act.wait_ge(probs_transposed, 2 * (N - 3))
                    h, s = n % GROUP, n // GROUP
                    nc.scalar.activation(probs[n % 4], SCORE[n % 2], ACT.Exp, scale=rq_now[:, h * TT + s:h * TT + s + 1],
                                         bias=neg_max[:, n % 4:n % 4 + 1], accum_out=row_sum[:, n % 4:n % 4 + 1])\
                        .then_inc(probs_ready, 1)
                    if n == 9:
                        act.wait_ge(wo_loaded, 16 * (g + 1))
                        wait_past(act, o_projected, g * TT)
                        copy(w_o[0], wo32, WSCALE, wo_hi)
                    if n == 15 and has_wq:
                        wq_part(g + 2)
                    if n in (7, 13) and not has_q:
                        expert_hi(n // 8, n // 8)

            attention(0, first=True)
            with act.Fori(1, KVH - 2) as g:
                attention(g)
            attention(KVH - 2, has_wq=False)
            attention(KVH - 1, has_q=False, has_wq=False)
            N = KVH * STEPS
            for n in range(LAG):
                transposed_hi(N - LAG + n, STEPS - LAG + n)
            out_hi(KVH * TT - 2, 0)
            out_hi(KVH * TT - 1, 1)

            for k in range(KD):
                act.wait_ge(ln_transposed, 2 * KD + k + 1)
                copy(xnT[0][:, k, :], LN_BANK2[k], 1.0, ln_hi)
            act.wait_ge(router_shifted, 2)
            for t in range(TT):
                nc.scalar.activation(rprob[:, t, :], logits[:, t, :], ACT.Exp, bias=r_neg[:, t:t + 1],
                                     accum_out=r_sum[:, t:t + 1]).then_inc(router_exp, 1)

            def expert(e, c, split=True):
                act.wait_ge(e_gate_done, e + 1)
                nc.scalar.activation(e_gate[c % 2], bank[4 + 2 * (c % 2)], ACT.Silu, scale=INV).then_inc(e_gate_act, 1)
                act.wait_ge(e_h_ready, e + 1)
                copy(e_hT[c % 2][0], e_h[c % 2], 1.0, e_h_hi)
                if split:
                    b = (c + 2) % 4
                    act.wait_ge(expert_loaded[b], loaded_after(e + 2, b))
                    copy(e_w[b][0], ew32[b], WSCALE, ew_hi)

            for e in range(2):
                expert(e, e)
            with act.Fori(0, (NE - 4) // 4) as i:
                for c in range(4):
                    expert(4 * i + 2 + c, (2 + c) % 4)
            for e in range(NE - 2, NE):
                expert(e, e % 4, split=False)

        @block.tensor
        def _(pe):
            def product(o, lhs, rhs, ks, done=None, first=True, last=True):
                n, total = 0, len(ks) * len(PARTS)
                for k in ks:
                    for a, b in PARTS:
                        m = nc.tensor.matmul(o, lhs(a, k), rhs(b, k), start=first and n == 0, stop=last and n == total - 1)
                        n += 1
                if done is not None:
                    m.then_inc(done, 1)

            def transpose_ln(banks):
                for k in range(KD):
                    for t in range(TT):
                        m = nc.tensor.transpose(banks[k][:, t * P:(t + 1) * P], xn[:, t, k * P:(k + 1) * P], ident[:, :])
                    m.then_inc(ln_transposed, 1)

            pe.wait_ge(consts_ready, 5 + NF)
            pe.wait_ge(x_quantised, 1)
            for k in range(KD):
                o = bank[4 + k][:, 0:TOK // 2].bitcast(bf16)
                for t in range(TT):
                    m = nc.tensor.transpose(o[:, t * P:(t + 1) * P], x_q[:, t, k * P:(k + 1) * P], ident16[:, :])
                m.then_inc(x_qT_psum, 1)
            pe.wait_ge(x_qT_ready, KD)
            for b in range(NB):
                pe.wait_ge(ctx_quantised, b + 1)
                for k in range(KD):
                    m = nc.tensor.matmul(bank[4 + b], ones16[:, :], ctx_q[:, b * KD + k, :], start=k == 0, stop=k == KD - 1)
                m.then_inc(colsum_done, 1)
                for t in range(2 * b, 2 * b + 2):
                    for k in range(KD):
                        m = nc.tensor.matmul(bank[t], x_qT[:, k, t * P:(t + 1) * P], ctx_q[:, b * KD + k, :],
                                             start=k == 0, stop=k == KD - 1)
                    m.then_inc(qprod_done, 1)
            pe.wait_ge(x_normed, 2 * TT)
            transpose_ln(LN_BANK0)

            def gate_up(u, b):
                pe.wait_ge(factors_applied, 2 * NF * (u + 1))
                wait_past(pe, h_ready, u)
                for o, c, done in ((GATE, 0, gate_done), (UP, D, up_done)):
                    for k in range(KD):
                        m = nc.tensor.matmul(o, w0[b][:, c + k * P:c + (k + 1) * P], xnT32[:, k, :], start=k == 0, stop=k == KD - 1)
                    m.then_inc(done, 1)

            def down(u, b):
                pe.wait_ge(h_ready, u + 1)
                first = isinstance(u, int) and u == 0
                for t in range(TT):
                    m = nc.tensor.matmul(DOWN[t], h0[b][:, t * P:(t + 1) * P], w0[b][:, 2 * D:3 * D], start=first, stop=True,
                                         skip_group_check=True)
                m.then_inc(down_done, 1)

            def project_values(z, src, banks, half=None):
                for h in range(2) if half is None else (half,):
                    product(banks[h], src, lambda b, k: w_v[b][:, k, h * 512:(h + 1) * 512], range(KD), v_projected)

            def project_keys(z, src):
                for h in range(2):
                    product((KV0, KV1)[h], src, lambda b, k: w_k[b][:, k, h * 512:(h + 1) * 512], range(KD), k_projected)

            def transpose_keys(z, banks):
                pe.wait_ge(k_normed, z + 1)
                for h in range(2):
                    for a in range(4):
                        m = nc.tensor.transpose(banks[h][:, a * P:(a + 1) * P], k_raw[:, 4 * h + a, :], ident[:, :])
                    m.then_inc(k_transposed, 1)

            def ctx_rows(z):
                return lambda a, k: ctxT[a][:, k, bass.ds(z * P, P)]

            def own_rows(t):
                return lambda a, k: xnT[a][:, k, t * P:(t + 1) * P]

            def pair(i, first):
                if first:
                    for done in (ctxT_hi, ctxT_split, wv_hi, wv_split):
                        pe.wait_ge(done, KD)
                    project_values(i, ctx_rows(i), (KV0, KV1))
                gate_up(2 * i, 0)
                if not first:
                    pe.wait_ge(k_copied, 2 * i)
                    project_values(i, ctx_rows(i), (KV0, KV1), 0)
                down(2 * i, 0)
                if not first:
                    project_values(i, ctx_rows(i), (KV0, KV1), 1)
                gate_up(2 * i + 1, 1)
                pe.wait_ge(v_hi, 2 * i + 2)
                pe.wait_ge(v_split, 2 * i + 2)
                if not first:
                    transpose_keys(i - 1, (KV0, KV1))
                down(2 * i + 1, 1)
                if first:
                    for done in (wk_hi, wk_split):
                        pe.wait_ge(done, KD)
                wait_past(pe, k_hi, 2 * i)
                wait_past(pe, k_split, 2 * i)
                project_keys(i, ctx_rows(i))

            pe.wait_ge(ln_hi, 2)
            pe.wait_ge(ln_ready, 2)
            pair(0, True)
            with pe.Fori(1, ITER) as i:
                pair(i, False)
            z = ITER
            project_values(z, ctx_rows(z), (GATE, UP))
            pe.wait_ge(v_hi, 2 * z + 2)
            pe.wait_ge(v_split, 2 * z + 2)
            pe.wait_ge(x_normed, 3 * TT)
            transpose_ln(LN_BANK1)
            pe.wait_ge(k_copied, 2 * z)
            project_keys(z, ctx_rows(z))
            transpose_keys(z - 1, (bank[0], bank[1]))
            pe.wait_ge(ln_hi, 2 + KD)
            pe.wait_ge(ln_ready, 2 + KD)
            for t in range(TT):
                z = CT + t
                wait_past(pe, v_hi, 2 * z)
                wait_past(pe, v_split, 2 * z)
                project_values(z, own_rows(t), (GATE, UP))
                pe.wait_ge(k_copied, 2 * z)
                project_keys(z, own_rows(t))
                pe.wait_ge(k_hi, 2 * z - 2)
                pe.wait_ge(k_split, 2 * z - 2)
                transpose_keys(z - 1, (bank[0], bank[1]))
            pe.wait_ge(k_hi, 2 * z)
            pe.wait_ge(k_split, 2 * z)
            transpose_keys(z, (bank[0], bank[1]))

            def project_queries(h, o):
                product(o, lambda a, k: w_q[a][:, k, h * HD:(h + 1) * HD], lambda b, k: xnT[b][:, k, :], range(KD), q_projected)

            def queries_read(count):
                for done in (q_hi, q_squared, q_split):
                    pe.wait_ge(done, count)

            def sum_squares(g, pair_):
                pe.wait_ge(q_squared, GROUP * g + 2 * pair_ + 2)
                wait_past(pe, sumsq_read, 2 * g + pair_)
                for h in range(2 * pair_, 2 * pair_ + 2):
                    for t in range(TT):
                        c = h * TT + t
                        m = nc.tensor.matmul(SUMSQ[:, c:c + 1], q_sq[:, h % 2, t * P:(t + 1) * P], ones[:, :], start=True, stop=True)
                m.then_inc(q_sumsq, 1)

            pe.wait_ge(wq_hi, 1)
            pe.wait_ge(wq_split, 1)
            pe.wait_ge(k_copied, 2 * (CT + TT))
            project_queries(0, Q0_BANK[0])
            project_queries(1, Q0_BANK[1])
            project_queries(2, Q0_BANK[2])
            sum_squares(0, 0)
            project_queries(3, Q0_BANK[3])
            for done in (k_hi, k_split, v_hi, v_split):
                pe.wait_ge(done, 2 * (CT + TT))

            def score(g, n):
                h, s = n % GROUP, n // GROUP
                b, N = s // 2, g * STEPS + n
                wait_past(pe, probs_ready, N - 1)
                if s == 0:
                    pe.wait_ge(q_hi, GROUP * g + h + 1)
                    pe.wait_ge(q_split, GROUP * g + h + 1)
                o, parts = SCORE[n % 2], len(PARTS)
                for p, (qa, kb) in enumerate(PARTS):
                    q = queries(g, qa, h, s)
                    nc.tensor.matmul(o[:, 0:CTX], q, key_head(KTc[kb], g, b * CTX, CTX), start=p == 0, stop=p == parts - 1)
                    m = nc.tensor.matmul(o[:, CTX:KEYS], q, key_head(KTl[kb], g, b * (KEYS - CTX), KEYS - CTX),
                                         start=p == 0, stop=p == parts - 1)
                m.then_inc(scores_ready, 1)

            def key_head(keys, g, start, size):
                return keys[:, bass.ds(g, 1), start:start + size].rearrange("p a n -> p (a n)")

            def transpose_probs(N, n):
                pe.wait_ge(probs_normed, N + 1)
                for c in range(2):
                    wait_past(pe, PT_hi, 2 * N + c - 1)
                    wait_past(pe, PT_split, 2 * N + c - 1)
                    for a in range(3):
                        k = 3 * c + a
                        m = nc.tensor.transpose(PT_BANK[c][:, a * P:(a + 1) * P], probs[n % 4][:, k * P:(k + 1) * P], ident[:, :])
                    m.then_inc(probs_transposed, 1)

            def attend(g, S, s, half):
                b = s // 2
                if half == 0:
                    wait_past(pe, o_hi, S)
                    wait_past(pe, o_split, S)
                    pe.wait_ge(PT_hi, 2 * GROUP * (S + 1))
                    pe.wait_ge(PT_split, 2 * GROUP * (S + 1))

                def value(a, k):
                    v = Vc[a][:, b * KD + k, :] if k < KD else Vl[a][:, b * 2 + k - KD, :]
                    return v[:, bass.ds(g * HD, HD)]

                product(O_BANK, value, lambda c, k: PT[s % 2][c][:, k, :], range(3 * half, 3 * half + 3),
                        o_done if half else None, first=half == 0, last=half == 1)

            def project_out(g, S, s):
                pe.wait_ge(o_hi, S + 1)
                pe.wait_ge(o_split, S + 1)
                if s == 0:
                    pe.wait_ge(wo_hi, g + 1)
                    pe.wait_ge(wo_split, g + 1)
                product(PROJ, lambda a, h: OT[s % 2][a][:, h, :], lambda b, h: w_o[b][:, h, :], range(GROUP), o_projected)

            def attention(g, first=False, has_q=True, has_s=True, steps=STEPS):
                for n in range(steps):
                    N = g * STEPS + n
                    if n == 0 and has_s:
                        wait_past(pe, PT_split, 2 * (N - 1 - LAG) + 1)
                        sum_squares(g, 1)
                    if n == 8 and has_q:
                        pe.wait_ge(PT_split, 2 * (N - 1 - LAG) + 1)
                        sum_squares(g + 1, 0)
                    if (not first or n >= LAG) and (has_s or n < LAG):
                        if (n == 1 and has_s) or (n == 9 and has_q):
                            wait_past(pe, sumsq_read, 2 * g + 2 if n == 1 else 2 * g + 3)
                        transpose_probs(N - LAG, (n - LAG) % STEPS)
                    if has_s:
                        score(g, n)
                    S = due(g, n, VALUES_0, first, not has_s)
                    if S is not None:
                        attend(g if n >= VALUES_0 else g - 1, S, (n - VALUES_0) // GROUP % TT, 0)
                    S = due(g, n, VALUES_1, first, not has_s)
                    if S is not None:
                        attend(g if n >= VALUES_1 else g - 1, S, (n - VALUES_1) // GROUP % TT, 1)
                    S = due(g, n, WO, first, not has_s)
                    if S is not None:
                        queries_read(GROUP * (g + 1) + n // GROUP if has_s and has_q else KVH * GROUP)
                        project_out(g if n >= WO else g - 1, S, (n - WO) // GROUP % TT)
                    if n % GROUP == 2 and has_q:
                        h = n // GROUP
                        if h == 0:
                            pe.wait_ge(wq_hi, g + 2)
                            pe.wait_ge(wq_split, g + 2)
                        if first and n < WO:
                            queries_read(GROUP * (g + 1) + h)
                        else:
                            pe.wait_ge(attn_added, g * TT + (n - WO + 2) // GROUP)
                        project_queries(h, PROJ)

            attention(0, first=True)
            with pe.Fori(1, KVH - 1) as g:
                attention(g)
            attention(KVH - 1, has_q=False)
            attention(KVH, has_q=False, has_s=False, steps=WO - 3)

            pe.wait_ge(x_normed, 4 * TT)
            transpose_ln(LN_BANK2)
            pe.wait_ge(ln_hi, 2 + 2 * KD)
            pe.wait_ge(ln_ready, 2 + 2 * KD)
            for t in range(TT):
                product(bank[0][:, t * EXPERTS:(t + 1) * EXPERTS], lambda a, k: xnT[a][:, k, t * P:(t + 1) * P],
                        lambda b, k: r_w[b][:, k, :], range(KD), logits_done)

            def expert_in(e, c):
                pe.wait_ge(ew_hi, e + 1)
                pe.wait_ge(ew_split, e + 1)
                wait_past(pe, e_h_ready, e - 1)
                for j, done in ((0, e_gate_done), (1, e_up_done)):
                    product(bank[4 + 2 * (c % 2) + j], lambda a, k: e_w[c][a][:, k * 2 * P + j * P:k * 2 * P + (j + 1) * P],
                            lambda b, k: xnT[b][:, k, :], range(KD), done)

            def expert_out(e, c):
                pe.wait_ge(e_h_hi, e + 1)
                pe.wait_ge(e_h_split, e + 1)
                for t in range(TT):
                    wait_past(pe, moe_added, TT * (e - 1) + t + 1 if not isinstance(e, int) or e > 0 else 0)
                    product(bank[t], lambda a, k: e_hT[c % 2][a][:, t * P:(t + 1) * P], lambda b, k: e_w[c][b][:, 2 * D:3 * D],
                            range(1), e_down_done)

            expert_in(0, 0)
            expert_in(1, 1)
            pe.wait_ge(logits_read, 1)
            expert_out(0, 0)
            with pe.Fori(0, (NE - 4) // 4) as i:
                for c in range(4):
                    e = 4 * i + 2 + c
                    expert_in(e, (2 + c) % 4)
                    expert_out(e - 1, (1 + c) % 4)
            for e in range(NE - 2, NE):
                expert_in(e, e % 4)
                expert_out(e - 1, (e - 1) % 4)
            expert_out(NE - 1, (NE - 1) % 4)

        @block.vector
        def _(dve):
            step = Steps(dve, dve_step)
            vec = nc.vector

            def rsqrt(y, v, t, done):
                n = step.did(vec.tensor_scalar(t.bitcast(i32), v.bitcast(i32), 1, None, ALU.logical_shift_right))
                yield
                step.wait(n)
                n = step.did(vec.tensor_scalar(y.bitcast(i32), t.bitcast(i32), -1.0, RSQRT_SEED, ALU.mult, ALU.add))
                for r in range(3):
                    yield
                    step.wait(n)
                    n = step.did(vec.scalar_tensor_tensor(t, y, -0.5, y, ALU.mult, ALU.mult))
                    yield
                    step.wait(n)
                    n = step.did(vec.tensor_tensor(t, t, v, ALU.mult))
                    yield
                    step.wait(n)
                    if r < 2:
                        n = step.did(vec.scalar_tensor_tensor(y, t, 1.5, y, ALU.add, ALU.mult))
                vec.scalar_tensor_tensor(y, t, 1.5, y, ALU.add, ALU.mult).then_inc(done, 1)

            def run(steps):
                for _ in steps:
                    pass

            ln_rstd = 0

            def layernorm():
                n = [step.did(vec.bn_stats(bn[:, t, :], x_res[:, t, :])) for t in range(TT)]
                for t in range(TT):
                    step.wait(n[t])
                    last = step.did(vec.bn_aggr(mv[:, t, :], bn[:, t, :]))
                step.wait(last)
                n = step.did(vec.tensor_scalar(ln_v[:, :], mv[:, :, 1], LN_EPS, None, ALU.add))
                step.wait(n)
                run(rsqrt(ln_r[:, :], ln_v[:, :], ln_t[:, :], ln_rstd_ready))
                nonlocal ln_rstd
                ln_rstd += 1
                dve.wait_ge(ln_rstd_ready, ln_rstd)
                for t in range(TT):
                    vec.tensor_scalar(xn[:, t, :], x_res[:, t, :], mv[:, t, 0:1], ln_r[:, t:t + 1], ALU.subtract, ALU.mult)\
                        .then_inc(x_normed, 1)

            def apply_factor(i, b, f):
                u = 2 * i + b
                dve.wait_ge(squares_ready, NF * u + f + 1)
                if f == 0:
                    dve.wait_ge(codes_scaled, u + 1)
                    wait_past(dve, down_done, u - 1)
                for c in range(2):
                    r = slice(c * HALF, (c + 1) * HALF)
                    if f > 0:
                        dve.wait_ge(factors_applied, 2 * (NF * u + f - 1) + c + 1)
                    vec.scalar_tensor_tensor(w0[b][:, r], square_buf[(NF * b + f) % 2][:, r], NF4_FACTORS[f][1],
                                             w0[b][:, r] if f else absmax_buf[b][:, r], ALU.add, ALU.mult)\
                        .then_inc(factors_applied, 1)

            dve.wait_ge(quant_loaded, 64)
            step.did(vec.reciprocal(qp[:, 0:1], quant_in[:, 0:1]))
            step.did(vec.reciprocal(qp[:, 1:2], quant_in[:, 2:3]))
            step.did(vec.tensor_scalar(qp[:, 2:3], quant_in[:, 1:2], -1.0, 128.0, ALU.mult, ALU.add))
            step.did(vec.tensor_scalar(qp[:, 3:4], quant_in[:, 3:4], -1.0, 128.0, ALU.mult, ALU.add))
            step.did(vec.tensor_tensor(qp[:, 4:5], quant_in[:, 0:1], quant_in[:, 2:3], ALU.mult))
            step.wait()
            n = step.did(vec.tensor_tensor(qp[:, 6:7], qp[:, 2:3], qp[:, 3:4], ALU.mult))
            step.wait(n)
            vec.tensor_scalar(qp[:, 5:6], qp[:, 6:7], float(D), None, ALU.mult).then_inc(quant_ready, 1)
            dve.wait_ge(x_loaded, 16)
            layernorm()

            def quantise(o, v, done):
                n = step.did(vec.tensor_scalar(v, v, ROUND, ROUND, ALU.add, ALU.max))
                step.wait(n)
                vec.tensor_scalar(o, v, ROUND + 255.0, ROUND + 128.0, ALU.min, ALU.subtract).then_inc(done, 1)

            dve.wait_ge(ctx_affine, 1)
            quantise(ctx_q[:, 0:KD, :], ctx32[:, 0:KD, :], ctx_quantised)
            dve.wait_ge(x_affine, TT)
            quantise(x_q, xn, x_quantised)
            dve.wait_ge(ctx_affine, 2)
            quantise(ctx_q[:, KD:2 * KD, :], ctx32[:, KD:2 * KD, :], ctx_quantised)
            dve.wait_ge(x_quantised, 1)
            n = step.did(vec.tensor_reduce(rowsum[:, :], x_q, AX, ALU.add))
            step.wait(n)
            dve.wait_ge(quant_ready, 1)
            n_row = step.did(vec.tensor_scalar(row_term[:, :], rowsum[:, :], qp[:, 3:4], qp[:, 5:6], ALU.mult, ALU.add))
            apply_factor(0, 0, 0)
            step.wait(n_row)
            for b in range(NB):
                dve.wait_ge(colsum_done, b + 1)
                n_col = step.did(vec.tensor_scalar(xn[:, b, :], bank[4 + b], qp[:, 2:3], None, ALU.mult))
                for t in range(2 * b, 2 * b + 2):
                    dve.wait_ge(qprod_done, t + 1)
                    step.wait(n_col)
                    v = xn[:, 2 + t % 2, :]
                    if b:
                        step.wait(n_add[t % 2])
                    else:
                        n_add = [0, 0]
                    n = step.did(vec.scalar_tensor_tensor(v, bank[t], row_term[:, t:t + 1], xn[:, b, :], ALU.add, ALU.add))
                    step.wait(n)
                    n_add[t % 2] = step.did(vec.scalar_tensor_tensor(x_res[:, t, :], v, qp[:, 4:5], x_res[:, t, :], ALU.mult, ALU.add))
            step.wait()
            layernorm()
            apply_factor(0, 0, 1)
            apply_factor(0, 0, 2)
            for k in range(1, KD, 2):
                dve.wait_ge(ln_transposed, k + 1)
                vec.tensor_copy(xnT32[:, k, :], LN_BANK0[k]).then_inc(ln_ready, 1)
            for f in range(3, NF):
                apply_factor(0, 0, f)

            def activate(u, b):
                dve.wait_ge(gate_activated, u + 1)
                dve.wait_ge(up_done, u + 1)
                vec.scalar_tensor_tensor(h0[b], UP, NF4_LEAD, gate_act, ALU.mult, ALU.mult).then_inc(h_ready, 1)

            def values_lo(z, hi, lo, banks):
                for h in range(2):
                    dve.wait_ge(v_hi, 2 * z + h + 1)
                    vec.scalar_tensor_tensor(lo(h), banks[h], INV, hi(h), ALU.mult, ALU.subtract).then_inc(v_split, 1)

            def key_rms(z):
                dve.wait_ge(k_squared, z + 1)
                n = step.did(vec.tensor_reduce(k_ss[:, :], k_sq, AX, ALU.add))
                yield
                step.wait(n)
                n = step.did(vec.tensor_scalar(k_v[:, :], k_ss[:, :], 1.0 / HD, RMS_EPS, ALU.mult, ALU.add))
                yield
                step.wait(n)
                yield from rsqrt(k_r[:, :], k_v[:, :], k_t[:, :], k_rstd)

            def keys_lo(z, hi, lo, banks):
                for h in range(2):
                    dve.wait_ge(k_hi, 2 * z + h + 1)
                    vec.scalar_tensor_tensor(lo(h), banks[h].rearrange("p (a b) -> p a b", a=4), w_qk[:, 0:1], hi(h),
                                             ALU.mult, ALU.subtract).then_inc(k_split, 1)

            def pair(i):
                n = i if isinstance(i, int) else 2
                if n > 0:
                    for f in range(NF):
                        apply_factor(i, 0, f)
                        if f == 0:
                            values_lo(i - 1, ctx_values(0, i - 1), ctx_values(1, i - 1), (KV0, KV1))
                        if f == 2:
                            activate(2 * i - 1, 1)
                        if f == 4 and n > 1:
                            keys_lo(i - 2, ctx_keys(0, i - 2), ctx_keys(1, i - 2), (KV0, KV1))
                norm = key_rms(i - 1) if n > 0 else iter(())
                for f in range(NF):
                    apply_factor(i, 1, f)
                    if f == 3:
                        activate(2 * i, 0)
                    if f > 1:
                        for _ in range(3):
                            next(norm, None)
                run(norm)

            dve.wait_ge(norms_loaded, 16)
            vec.tensor_tensor(w_qk[:, :], norm_in[:, 0:1], norm_in[:, 1:2], ALU.mult).then_inc(w_qk_ready, 1)
            dve.wait_ge(router_loaded, 32)
            n = step.did(vec.tensor_scalar(r_w[0][:, :, :], rw32[:, :, :], WSCALE, None, ALU.mult))
            step.wait(n)
            step.did(vec.scalar_tensor_tensor(r_w[1][:, :, :], rw32[:, :, :], WSCALE, r_w[0][:, :, :], ALU.mult, ALU.subtract))
            pair(0)
            pair(1)
            base = step.base + step.k
            step.at(base)
            PER_PAIR = 12
            with dve.Fori(2, ITER) as i:
                step.at((i - 2) * PER_PAIR + base)
                pair(i)
                assert step.k == PER_PAIR, step.k
            step.at(base + (ITER - 2) * PER_PAIR)
            z = ITER - 1
            values_lo(z, ctx_values(0, z), ctx_values(1, z), (KV0, KV1))
            activate(UNITS - 1, 1)
            keys_lo(z - 1, ctx_keys(0, z - 1), ctx_keys(1, z - 1), (KV0, KV1))
            dve.wait_ge(down_done, UNITS)
            for t in range(TT):
                vec.scalar_tensor_tensor(x_res[:, t, :], DOWN[t], NF4_LEAD, x_res[:, t, :], ALU.mult, ALU.add).then_inc(ffn_added, 1)
            dve.wait_ge(ffn_added, TT)
            layernorm()
            values_lo(z + 1, ctx_values(0, z + 1), ctx_values(1, z + 1), (GATE, UP))

            def ln_lo(done, banks):
                for k in range(KD):
                    dve.wait_ge(ln_hi, done + k + 1)
                    vec.tensor_tensor(xnT[1][:, k, :], banks[k], xnT[0][:, k, :], ALU.subtract).then_inc(ln_ready, 1)

            ln_lo(2, LN_BANK1)
            run(key_rms(z))
            keys_lo(z, ctx_keys(0, z), ctx_keys(1, z), (bank[0], bank[1]))
            run(key_rms(z + 1))

            def wq_lo(g):
                dve.wait_ge(wq_hi, g + 1)
                vec.scalar_tensor_tensor(flat(w_q[1]), flat(wq32), WSCALE, flat(w_q[0]), ALU.mult, ALU.subtract).then_inc(wq_split, 1)

            wq_lo(0)
            for t in range(TT):
                z = CT + t
                values_lo(z, own_values(0, t), own_values(1, t), (GATE, UP))
                if t:
                    keys_lo(z - 1, own_keys(0, t - 1), own_keys(1, t - 1), (bank[0], bank[1]))
                else:
                    keys_lo(z - 1, ctx_keys(0, z - 1), ctx_keys(1, z - 1), (bank[0], bank[1]))
                run(key_rms(z))
            keys_lo(z, own_keys(0, TT - 1), own_keys(1, TT - 1), (bank[0], bank[1]))

            def query_lo(g, h, src):
                dve.wait_ge(q_squared, GROUP * g + h + 1)
                vec.scalar_tensor_tensor(queries(g, 1, h), src, INV, queries(g, 0, h), ALU.mult, ALU.subtract).then_inc(q_split, 1)

            def query_rms(g, pair_):
                dve.wait_ge(q_sumsq, 2 * g + pair_ + 1)
                c = slice(pair_ * 2 * TT, (pair_ + 1) * 2 * TT)
                vec.tensor_scalar(rq_v[:, c], SUMSQ[:, c], 1.0 / HD, RMS_EPS, ALU.mult, ALU.add).then_inc(sumsq_read, 1)
                dve.wait_ge(sumsq_read, 2 * g + pair_ + 1)
                return rsqrt(rq_next[:, c], rq_v[:, c], rq_t[:, c], rq_ready)

            def use_query_rms(g, pair_):
                dve.wait_ge(rq_ready, 2 * g + pair_ + 1)
                c = slice(pair_ * 2 * TT, (pair_ + 1) * 2 * TT)
                return step.did(vec.tensor_scalar(rq_now[:, c], rq_next[:, c], HD ** -0.5, None, ALU.mult))

            for h in range(3):
                query_lo(0, h, Q0_BANK[h])
            run(query_rms(0, 0))
            query_lo(0, 3, Q0_BANK[3])
            wq_lo(1)

            def row_maximum(N, n, wait_for):
                h, s = n % GROUP, n // GROUP
                dve.wait_ge(scores_ready, N + 1)
                c = slice(n % 4, n % 4 + 1)
                m = step.did(vec.tensor_reduce(row_max[:, c], SCORE[n % 2], AX, ALU.max))
                if wait_for is not None:
                    step.wait(wait_for)
                return m

            def negate_maximum(n, m):
                h, s = n % GROUP, n // GROUP
                c = slice(n % 4, n % 4 + 1)
                step.wait(m)
                vec.tensor_scalar(neg_max[:, c], row_max[:, c], rq_now[:, h * TT + s:h * TT + s + 1], -1.0, ALU.mult, ALU.mult)\
                    .then_inc(neg_max_ready, 1)

            def invert_sum(N, n):
                dve.wait_ge(probs_ready, N + 1)
                c = slice(n % 4, n % 4 + 1)
                vec.reciprocal(inv_sum[:, c], row_sum[:, c]).then_inc(sum_inverted, 1)

            def transposed_lo(N, n):
                for c in range(2):
                    dve.wait_ge(PT_hi, 2 * N + c + 1)
                    vec.tensor_tensor(PT_slot(1, n, c), PT_BANK[c][:, 0:3 * P].rearrange("p (a b) -> p a b", a=3),
                                      PT_slot(0, n, c), ALU.subtract).then_inc(PT_split, 1)

            def out_lo(S, s):
                dve.wait_ge(o_hi, S + 1)
                vec.tensor_tensor(flat(OT[s % 2][1]), O_BANK, flat(OT[s % 2][0]), ALU.subtract).then_inc(o_split, 1)

            def add_attention(S, s):
                dve.wait_ge(o_projected, S + 1)
                vec.scalar_tensor_tensor(x_res[:, s, :], PROJ, INV, x_res[:, s, :], ALU.mult, ALU.add).then_inc(attn_added, 1)

            def expert_lo(e, b):
                dve.wait_ge(ew_hi, e + 1)
                vec.scalar_tensor_tensor(e_w[b][1], ew32[b], WSCALE, e_w[b][0], ALU.mult, ALU.subtract).then_inc(ew_split, 1)

            def attention(g, first=False, has_q=True, has_wq=True):
                for n in range(STEPS):
                    N = g * STEPS + n
                    if not first or n:
                        invert_sum(N - 1, (n - 1) % STEPS)
                    S = due(g, n, OUT, first)
                    if S is not None:
                        out_lo(S, (n - OUT) // GROUP)
                    if n % GROUP == 3 and has_q:
                        query_lo(g + 1, n // GROUP, PROJ)
                    S = due(g, n, ADD, first)
                    if S is not None:
                        add_attention(S, (n - ADD) // GROUP % TT)
                    if not first or n >= LAG:
                        transposed_lo(N - LAG, (n - LAG) % STEPS)
                    used = use_query_rms(g, n // 2) if n in (0, 2) else None
                    m = row_maximum(N, n, used)
                    negate_maximum(n, m)
                    if n == 0:
                        run(query_rms(g, 1))
                    if n == 8 and has_q:
                        run(query_rms(g + 1, 0))
                    if n == 10:
                        dve.wait_ge(wo_hi, g + 1)
                        vec.scalar_tensor_tensor(flat(w_o[1]), flat(wo32), WSCALE, flat(w_o[0]), ALU.mult, ALU.subtract)\
                            .then_inc(wo_split, 1)
                    if n == 15 and has_wq:
                        wq_lo(g + 2)
                    if n in (7, 13) and not has_q:
                        expert_lo(n // 8, n // 8)

            attention(0, first=True)
            base = step.base + step.k
            PER_GROUP = STEPS + 2 + 2 * 10
            with dve.Fori(1, KVH - 2) as g:
                step.at((g - 1) * PER_GROUP + base)
                attention(g)
                assert step.k == PER_GROUP, step.k
            step.at(base + (KVH - 3) * PER_GROUP)
            attention(KVH - 2, has_wq=False)
            attention(KVH - 1, has_q=False, has_wq=False)
            N = KVH * STEPS
            invert_sum(N - 1, STEPS - 1)
            for n in range(LAG):
                transposed_lo(N - LAG + n, STEPS - LAG + n)
            add_attention(KVH * TT - 3, 1)
            out_lo(KVH * TT - 2, 0)
            add_attention(KVH * TT - 2, 2)
            out_lo(KVH * TT - 1, 1)
            add_attention(KVH * TT - 1, 3)
            dve.wait_ge(attn_added, KVH * TT)
            dve.wait_ge(wo_split, KVH)
            layernorm()
            ln_lo(2 + KD, LN_BANK2)

            dve.wait_ge(logits_done, TT)
            vec.tensor_scalar(logits, bank[0][:, 0:TT * EXPERTS].rearrange("p (t e) -> p t e", t=TT), INV, None, ALU.mult)\
                .then_inc(logits_read, 1)
            dve.wait_ge(logits_read, 1)
            vec.tensor_reduce(r_max[:, :], logits, AX, ALU.max).then_inc(router_shifted, 1)
            dve.wait_ge(router_shifted, 1)
            vec.tensor_scalar(r_neg[:, :], r_max[:, :], -1.0, None, ALU.mult).then_inc(router_shifted, 1)
            dve.wait_ge(router_exp, TT)
            n = step.did(vec.reciprocal(r_inv[:, :], r_sum[:, :]))
            step.wait(n)
            ns = [step.did(vec.tensor_scalar(rprob[:, t, :], rprob[:, t, :], r_inv[:, t:t + 1], None, ALU.mult)) for t in range(TT)]
            nm = []
            for t in range(TT):
                step.wait(ns[t])
                nm.append(step.did(vec.max(out=top8[:, t, :], in_=rprob[:, t, :])))
            for t in range(TT):
                step.wait(nm[t])
                n = step.did(vec.max_index(top8i[:, t, :], top8[:, t, :], rprob[:, t, :]))
            step.did(vec.tensor_tensor(r_sum[:, :], top8[:, :, 0], top8[:, :, 1], ALU.add))
            step.wait()
            step.did(vec.tensor_copy(top_i[:, :, :], top8i[:, :, 0:2]))
            n = step.did(vec.reciprocal(r_max[:, :], r_sum[:, :]))
            step.wait(n)
            n = step.did(vec.tensor_tensor(top_w[:, :, :], top8[:, :, 0:2], r_max[:, :, None].to_broadcast((P, TT, 2)), ALU.mult))
            step.wait(n)
            for t in range(TT):
                for c in range(2):
                    n = step.did(vec.tensor_scalar(pick[:, t, c, :], iota_in[:, :], top_i[:, t, c:c + 1], top_w[:, t, c:c + 1],
                                                   ALU.is_equal, ALU.mult))
            step.wait(n)
            n = step.did(vec.tensor_tensor(logits, pick[:, :, 0, :], pick[:, :, 1, :], ALU.add))
            step.wait(n)
            dve.wait_ge(consts_ready, 3)
            vec.tensor_scalar(combine[:, :, SHARED:NE], logits, INV, None, ALU.mult).then_inc(combine_ready, 1)
            dve.wait_ge(combine_ready, 1)

            def add_expert(e, column):
                for t in range(TT):
                    dve.wait_ge(e_down_done, TT * e + t + 1)
                    wait_past(dve, moe_added, TT * (e - 1) + t + 1 if not isinstance(e, int) or e > 0 else 0)
                    vec.scalar_tensor_tensor(x_res[:, t, :], bank[t], column(t), x_res[:, t, :], ALU.mult, ALU.add)\
                        .then_inc(moe_added, 1)

            def expert(e, c, split=True, add=True):
                dve.wait_ge(e_gate_act, e + 1)
                dve.wait_ge(e_up_done, e + 1)
                vec.scalar_tensor_tensor(e_h[c % 2], bank[5 + 2 * (c % 2)], INV, e_gate[c % 2], ALU.mult, ALU.mult).then_inc(e_h_ready, 1)
                if split:
                    expert_lo(e + 2, (c + 2) % 4)
                dve.wait_ge(e_h_hi, e + 1)
                vec.tensor_tensor(e_hT[c % 2][1], e_h[c % 2], e_hT[c % 2][0], ALU.subtract).then_inc(e_h_split, 1)
                if add:
                    add_expert(e - 1, lambda t: combine[:, t, bass.ds(e - 1, 1)])

            expert(0, 0, add=False)
            expert(1, 1)
            with dve.Fori(0, (NE - 4) // 4) as i:
                for c in range(4):
                    expert(4 * i + 2 + c, (2 + c) % 4)
            for e in range(NE - 2, NE):
                expert(e, e % 4, split=False)
            add_expert(NE - 1, lambda t: combine[:, t, NE - 1:NE])


def kernel(x, ctx_4096, L0_xattn_x1_scale, L0_xattn_x1_zp, L0_xattn_x2_scale, L0_xattn_x2_zp, L0_ffn_gate_q,
           L0_ffn_gate_absmax, L0_ffn_up_q, L0_ffn_up_absmax, L0_ffn_down_q, L0_ffn_down_absmax, L1_xattn_Wq, L1_xattn_Wk,
           L1_xattn_Wv, L1_xattn_Wo, L1_xattn_q_norm_w, L1_xattn_k_norm_w, L1_ffn_gate_w, L1_ffn_w_gate_up, L1_ffn_w_down,
           L1_ffn_shared_w_gate_up, L1_ffn_shared_w_down):
    import numpy as np
    import concourse.bacc as bacc
    from concourse.bass_utils import run_bass_kernel_spmd

    a = np.ascontiguousarray
    f = np.asarray
    ctx = f(ctx_4096).reshape(NB * CTX, D)

    def by_unit(w):
        return f(w).reshape(UNITS, P, KD, P).transpose(0, 3, 2, 1).reshape(UNITS, P, D)

    def by_unit_absmax(s):
        return f(s).reshape(UNITS, P, KD, 2).transpose(0, 3, 2, 1).reshape(UNITS, 2, D)

    codes = np.concatenate([by_unit(L0_ffn_gate_q), by_unit(L0_ffn_up_q),
                            f(L0_ffn_down_q).T.reshape(UNITS, P, D)], axis=2)
    absmax = np.concatenate([by_unit_absmax(L0_ffn_gate_absmax), by_unit_absmax(L0_ffn_up_absmax),
                             f(L0_ffn_down_absmax).reshape(D, UNITS, 2).transpose(1, 2, 0)], axis=2)

    def expert_in(gate, up):
        both = np.stack([gate, up], axis=1).reshape(-1, 2, INTER, KD, P)
        return both.transpose(0, 4, 3, 1, 2).reshape(-1, P, KD * 2 * INTER)

    gu, sgu = f(L1_ffn_w_gate_up), f(L1_ffn_shared_w_gate_up).reshape(2, SHARED, INTER, D)
    experts = np.concatenate([
        np.concatenate([expert_in(sgu[0], sgu[1]), f(L1_ffn_shared_w_down).T.reshape(SHARED, INTER, D)], axis=2),
        np.concatenate([expert_in(gu[:, :INTER], gu[:, INTER:]), f(L1_ffn_w_down).transpose(0, 2, 1)], axis=2)], axis=0)
    ins = [
        ("x", f(x).reshape(TOK, D)),
        ("ctx", ctx),
        ("ctx_t", ctx.T),
        ("quant", np.stack([f(L0_xattn_x1_scale), f(L0_xattn_x1_zp), f(L0_xattn_x2_scale), f(L0_xattn_x2_zp)])),
        ("codes", codes),
        ("absmax", absmax),
        ("wk", f(L1_xattn_Wk)),
        ("wv", f(L1_xattn_Wv)),
        ("wq", f(L1_xattn_Wq)),
        ("wo", f(L1_xattn_Wo)),
        ("norms", np.stack([f(L1_xattn_q_norm_w), f(L1_xattn_k_norm_w)], axis=1)),
        ("router_w", f(L1_ffn_gate_w).T),
        ("experts", experts),
        ("iota", np.tile(np.arange(EXPERTS, dtype=np.float32), (P, 1))),
    ]
    nc = bacc.Bacc("TRN2", target_bir_lowering=False, num_devices=1)
    arrays, args = {}, []
    for name, v in ins:
        v = a(v)
        arrays[name] = v
        args.append(nc.dram_tensor(name, v.shape, mybir.dt.from_np(v.dtype), kind="ExternalInput").ap())
    args.append(nc.dram_tensor("out", (TOK, D), mybir.dt.float32, kind="ExternalOutput").ap())
    bass_xattn_ffn_two_layers(nc, *args)
    r = run_bass_kernel_spmd(nc, [arrays], core_ids=[0])
    return r.results[0]["out"].reshape(NB, TOK // NB, D)
```

```python
import concourse.bass as bass
from concourse import mybir
from contextlib import ExitStack

P = 128
TOK, D, NB = 512, 512, 2
CTX = 512
TT, KD = TOK // P, D // P
CT = NB * CTX // P
FF = 1792
UNITS = FF // P
HEADS, KVH, HD = 32, 8, 128
GROUP = HEADS // KVH
KEYS = CTX + TOK // NB
KB = KEYS // P
EXPERTS, SHARED, INTER = 16, 4, 128
NE = EXPERTS + SHARED
WSCALE = 64.0
INV = 1.0 / WSCALE
LN_EPS, RMS_EPS = 1e-5, 1e-6
ROUND = 12582912.0
RSQRT_SEED = 1597463007.0

NF4_LEAD = 0.003969766543852396
NF4_FACTORS = [
    (-0.035814158618450165, 0.01144565548747778), (-3.722414255142212, 0.013174708932638168),
    (-0.4697154760360718, 0.1573619842529297), (-3.2984719276428223, 0.1701432317495346),
    (-1.0957497358322144, 0.33853575587272644), (-2.6926143169403076, 0.37515297532081604),
    (-1.9447404146194458, 0.3761288523674011)]
NF = len(NF4_FACTORS)
UNIT = 3 * D
HALF = UNIT // 2
ITER = UNITS // 2


class Steps:

    def __init__(self, eng, sem):
        self.eng, self.sem, self.base, self.k = eng, sem, 0, 0

    def did(self, instruction):
        instruction.then_inc(self.sem, 1)
        self.k += 1
        return self.base + self.k

    def wait(self, value=None):
        self.eng.wait_ge(self.sem, self.base + self.k if value is None else value)

    def at(self, base):
        self.base, self.k = base, 0


def wait_past(eng, sem, value):
    if not isinstance(value, int) or value > 0:
        eng.wait_ge(sem, value)


def bass_xattn_ffn_two_layers(nc, x, ctx, ctx_t, quant, codes, absmax, wk, wv, wq, wo, norms,
                              router_w, experts, iota, out):
    f32, f16, bf16 = mybir.dt.float32, mybir.dt.float16, mybir.dt.bfloat16
    i32, u32 = mybir.dt.int32, mybir.dt.uint32
    ALU, ACT, AX = mybir.AluOpType, mybir.ActivationFunctionType, mybir.AxisListType.X

    ctxs = ExitStack()
    with ctxs:
        arena = ctxs.enter_context(nc.sbuf_tensor("arena", [P, 204 * 256], f32))

        def place(kib, shape, dtype=f32):
            n = 1
            for s in shape:
                n *= s
            words = n if dtype in (f32, i32) else n // 2
            start = int(kib * 256)
            v = arena[:, start:start + words]
            if dtype is not f32:
                v = v.bitcast(dtype)
            if len(shape) == 2:
                v = v.rearrange("p (a b) -> p a b", a=shape[0])
            if len(shape) == 3:
                v = v.rearrange("p (a b c) -> p a b c", a=shape[0], b=shape[1])
            return v

        x_res = place(0, (TT, D))
        xn = place(112, (TT, D))
        xnT32 = place(120, (KD, TOK))
        xnT = [place(120, (KD, TOK), f16), place(124, (KD, TOK), f16)]
        KTc = [place(8, (KVH, NB * CTX), f16), place(24, (KVH, NB * CTX), f16)]
        Vc = [place(40, (CT, KVH * HD), f16), place(56, (CT, KVH * HD), f16)]
        KTl = [place(128, (KVH, TOK), f16), place(136, (KVH, TOK), f16)]
        Vl = [place(144, (TT, KVH * HD), f16), place(152, (TT, KVH * HD), f16)]
        w_k = [place(72, (KD, KVH * HD), f16), place(80, (KD, KVH * HD), f16)]
        w_v = [place(88, (KD, KVH * HD), f16), place(96, (KD, KVH * HD), f16)]
        k_raw = place(104, (KVH, HD))
        k_sq = place(108, (KVH, HD))
        ctx32 = place(8, (CT, D))
        ctxT32 = place(40, (KD, NB * CTX))
        wk32 = place(24, (KD, KVH * HD))
        wv32 = place(56, (KD, KVH * HD))
        ctxT = [place(128, (KD, NB * CTX), f16), place(136, (KD, NB * CTX), f16)]
        ctx_q = place(104, (CT, D), bf16)
        x_q = place(144, (TT, D), bf16)
        x_qT = place(156, (KD, TOK), bf16)
        h0 = [place(144, (TOK,)), place(146, (TOK,))]
        w0 = [place(148, (UNIT,)), place(154, (UNIT,))]
        code_buf = [place(160, (UNIT,), i32), place(166, (UNIT,), i32)]
        absmax_buf = [place(172, (UNIT,)), place(178, (UNIT,))]
        square_buf = [place(184, (UNIT,)), place(190, (UNIT,))]
        gate_act = place(196, (TOK,))
        shifted = place(198, (UNIT,))
        PT = [[place(72 + 12 * b + 6 * v, (KB, GROUP * P), f16) for v in range(2)] for b in range(2)]
        probs = [place(96 + 3 * b, (KEYS,)) for b in range(4)]
        OT = [[place(108 + 2 * b + v, (GROUP, P), f16) for v in range(2)] for b in range(2)]
        wo32 = place(112, (GROUP, D))
        QT = place(160, (2, 2, GROUP * TOK), f16)
        wq32 = place(176, (KD, GROUP * HD))
        w_q = [place(184, (KD, GROUP * HD), f16), place(188, (KD, GROUP * HD), f16)]
        w_o = [place(192, (GROUP, D), f16), place(196, (GROUP, D), f16)]
        q_sq = place(200, (2, TOK))
        EW = 3 * D
        ew32 = [place(k, (EW,)) for k in (176, 182, 8, 14)]
        e_w = [[place(k, (EW,), f16), place(m, (EW,), f16)] for k, m in ((160, 163), (188, 200), (20, 23), (26, 29))]
        e_gate = [place(50 + 2 * b, (TOK,)) for b in range(2)]
        e_h = [place(54 + 2 * b, (TOK,)) for b in range(2)]
        e_hT = [[place(58 + 2 * b + v, (TOK,), f16) for v in range(2)] for b in range(2)]

        def small(name, shape, dtype=f32):
            return ctxs.enter_context(nc.sbuf_tensor(name, shape, dtype))

        ident = small("ident", [P, P])
        ident16 = small("ident16", [P, P], bf16)
        ones16 = small("ones16", [P, P], bf16)
        ones = small("ones", [P, 1])
        factor_b = small("factor_b", [P, NF])
        turn = small("turn", [P, 2])
        quant_in = small("quant_in", [P, 4])
        qp = small("qp", [P, 8])
        row_term = small("row_term", [P, TT])
        norm_in = small("norm_in", [P, 2])
        w_qk = small("w_qk", [P, 1])
        bn = small("bn", [P, TT, 6])
        mv = small("mv", [P, TT, 2])
        ln_r = small("ln_r", [P, TT])
        ln_v = small("ln_v", [P, TT])
        ln_t = small("ln_t", [P, TT])
        k_ss = small("k_ss", [P, KVH])
        k_r = small("k_r", [P, KVH])
        k_v = small("k_v", [P, KVH])
        k_t = small("k_t", [P, KVH])
        rq_next = small("rq_next", [P, GROUP * TT])
        rq_v = small("rq_v", [P, GROUP * TT])
        rq_t = small("rq_t", [P, GROUP * TT])
        rq_now = small("rq_now", [P, GROUP * TT])
        row_max = small("row_max", [P, 4])
        neg_max = small("neg_max", [P, 4])
        row_sum = small("row_sum", [P, 4])
        inv_sum = small("inv_sum", [P, 4])
        rw32 = small("rw32", [P, KD, EXPERTS])
        r_w = [small("r_w_hi", [P, KD, EXPERTS], f16), small("r_w_lo", [P, KD, EXPERTS], f16)]
        iota_in = small("iota_in", [P, EXPERTS])
        logits = place(62, (TT, EXPERTS))
        rprob = place(62.25, (TT, EXPERTS))
        r_max = small("r_max", [P, TT])
        r_neg = small("r_neg", [P, TT])
        r_sum = small("r_sum", [P, TT])
        r_inv = small("r_inv", [P, TT])
        top8 = small("top8", [P, TT, 8])
        top8i = small("top8i", [P, TT, 8], u32)
        top_i = small("top_i", [P, TT, 2])
        top_w = small("top_w", [P, TT, 2])
        pick = place(62.5, (TT, 2, EXPERTS))
        combine = small("combine", [P, TT, NE])

        psum = ctxs.enter_context(nc.psum_tensor("psum", [P, 8 * 512], f32))
        bank = [psum[:, b * 512:(b + 1) * 512] for b in range(8)]
        DOWN, GATE, UP, KV0, KV1 = bank[0:4], bank[4], bank[5], bank[6], bank[7]
        SCORE = [psum[:, 0:KEYS], psum[:, 1024:1024 + KEYS]]
        PT_BANK = bank[4:6]
        O_BANK, PROJ = bank[6], bank[7]
        ROWSUM = bank[6][:, 0:TT]
        LAST_O, LAST_PROJ = bank[0], bank[2]
        SUMSQ = PT_BANK[0][:, 3 * P:3 * P + GROUP * TT]
        LN_BANK0, LN_BANK1, LN_BANK2 = bank[0:4], (bank[2], bank[3], bank[4], bank[5]), bank[4:8]
        Q0_BANK = (bank[2], bank[3], bank[7], bank[6])

        def sem(name):
            return ctxs.enter_context(nc.semaphore(name))

        quant_loaded, norms_loaded, x_loaded = map(sem, ("quant_loaded", "norms_loaded", "x_loaded"))
        ctx_loaded = [sem("ctx_loaded0"), sem("ctx_loaded1")]
        ctxT_loaded, wk_loaded, wv_loaded, router_loaded = map(sem, ("ctxT_loaded", "wk_loaded", "wv_loaded", "router_loaded"))
        codes_loaded = [sem("codes_loaded0"), sem("codes_loaded1")]
        absmax_loaded = [sem("absmax_loaded0"), sem("absmax_loaded1")]
        wq_loaded, wo_loaded = sem("wq_loaded"), sem("wo_loaded")
        expert_loaded = [sem(f"expert_loaded{b}") for b in range(4)]
        stored = sem("stored")
        dve_step, pool_step = sem("dve_step"), sem("pool_step")
        consts_ready, quant_ready, x_normed, x_affine, ctx_affine = map(sem, ("consts_ready", "quant_ready", "x_normed", "x_affine", "ctx_affine"))
        x_quantised, ctx_quantised, x_qT_psum, x_qT_ready = map(sem, ("x_quantised", "ctx_quantised", "x_qT_psum", "x_qT_ready"))
        rowsum_done, colsum_done, qprod_done = sem("rowsum_done"), sem("colsum_done"), sem("qprod_done")
        ctxT_hi, ctxT_split, wk_hi, wk_split, wv_hi, wv_split = map(sem, ("ctxT_hi", "ctxT_split", "wk_hi", "wk_split", "wv_hi", "wv_split"))
        ln_transposed, ln_hi, ln_ready, ln_rstd_ready, w_qk_ready = map(sem, ("ln_transposed", "ln_hi", "ln_ready", "ln_rstd_ready", "w_qk_ready"))
        turn_set = sem("turn_set")
        codes_shifted, codes_scaled, squares_ready, factors_applied = map(sem, ("codes_shifted", "codes_scaled", "squares_ready", "factors_applied"))
        gate_done, up_done, gate_activated, h_ready, down_done = map(sem, ("gate_done", "up_done", "gate_activated", "h_ready", "down_done"))
        ffn_added = sem("ffn_added")
        k_projected, k_copied, k_squared, k_rstd, k_normed = map(sem, ("k_projected", "k_copied", "k_squared", "k_rstd", "k_normed"))
        k_transposed, k_hi, k_split, v_projected, v_hi, v_split = map(sem, ("k_transposed", "k_hi", "k_split", "v_projected", "v_hi", "v_split"))
        wq_hi, wq_split, wo_hi, wo_split = map(sem, ("wq_hi", "wq_split", "wo_hi", "wo_split"))
        q_projected, q_hi, q_squared, q_split, q_sumsq, sumsq_read, rq_ready = map(sem, ("q_projected", "q_hi", "q_squared", "q_split", "q_sumsq", "sumsq_read", "rq_ready"))
        scores_ready, neg_max_ready, probs_ready, sum_inverted, probs_normed = map(sem, ("scores_ready", "neg_max_ready", "probs_ready", "sum_inverted", "probs_normed"))
        probs_transposed, PT_hi, PT_split = sem("probs_transposed"), sem("PT_hi"), sem("PT_split")
        o_done, o_hi, o_split, o_projected, attn_added = map(sem, ("o_done", "o_hi", "o_split", "o_projected", "attn_added"))
        logits_done, logits_read, router_shifted, router_exp, combine_ready = map(sem, ("logits_done", "logits_read", "router_shifted", "router_exp", "combine_ready"))
        ew_hi, ew_split, e_gate_done, e_up_done, e_gate_act = map(sem, ("ew_hi", "ew_split", "e_gate_done", "e_up_done", "e_gate_act"))
        e_h_ready, e_h_hi, e_h_split, e_down_done, moe_added = map(sem, ("e_h_ready", "e_h_hi", "e_h_split", "e_down_done", "moe_added"))

        block = ctxs.enter_context(nc.Block())

        PARTS = ((0, 0), (0, 1), (1, 0))
        STEPS = GROUP * TT

        VALUES_0, VALUES_1, OUT, WO, ADD = 7, 9, 10, 12, 13
        LAG = 2

        def due(g, n, delay, first=False):
            if (n - delay) % GROUP or (first and n < delay):
                return None
            return g * TT + (n - delay) // GROUP

        def flat(v):
            return v.rearrange("p a b -> p (a b)")

        def ctx_values(part, z):
            return lambda h: Vc[part][:, bass.ds(z, 1), h * 512:(h + 1) * 512].rearrange("p a n -> p (a n)")

        def own_values(part, t):
            return lambda h: Vl[part][:, t, h * 512:(h + 1) * 512]

        def ctx_keys(part, z):
            return lambda h: KTc[part][:, 4 * h:4 * h + 4, bass.ds(z * P, P)]

        def own_keys(part, t):
            return lambda h: KTl[part][:, 4 * h:4 * h + 4, t * P:(t + 1) * P]

        def queries(g, part, h, s=None):
            start, size = (h * TOK, TOK) if s is None else (h * TOK + s * P, P)
            return QT[:, bass.ds(g % 2, 1), part, start:start + size].rearrange("p a n -> p (a n)")

        def PT_slot(part, n, c):
            return PT[(n // GROUP) % 2][part][:, 3 * c:3 * c + 3, (n % GROUP) * P:(n % GROUP + 1) * P]

        def loaded_after(e, b):
            return (e - b) * 4 + 16

        @block.sync
        def _(sp):
            def load_unit(i, b):
                u = 2 * i + b
                wait_past(sp, squares_ready, NF * (u - 1))
                row = bass.ds(u, 1)
                sp.dma_start(code_buf[b], codes[row, :, :].rearrange("a p n -> p (a n)")).then_inc(codes_loaded[b], 16)
                sp.dma_start(absmax_buf[b], absmax[row, :, :].rearrange("a h n -> h a n").to_broadcast((2, P // 2, UNIT)))\
                    .then_inc(absmax_loaded[b], 16)

            sp.dma_start(x_res, x.rearrange("(t p) n -> p t n", p=P)).then_inc(x_loaded, 16)
            for c in range(4):
                sp.dma_start(quant_in[:, c:c + 1], quant[c:c + 1, :].to_broadcast((P, 1))).then_inc(quant_loaded, 16)
            for b in range(NB):
                sp.dma_start(ctx32[:, b * KD:(b + 1) * KD, :], ctx[b * CTX:(b + 1) * CTX, :].rearrange("(t p) n -> p t n", p=P))\
                    .then_inc(ctx_loaded[b], 16)
            load_unit(0, 0)
            sp.dma_start(ctxT32, ctx_t.rearrange("(k p) n -> p k n", p=P)).then_inc(ctxT_loaded, 16)
            sp.dma_start(wv32, wv.rearrange("(k p) n -> p k n", p=P)).then_inc(wv_loaded, 16)
            sp.dma_start(wk32, wk.rearrange("(k p) n -> p k n", p=P)).then_inc(wk_loaded, 16)
            sp.dma_start(norm_in[:, :], norms).then_inc(norms_loaded, 16)
            sp.dma_start(rw32[:, :, :], router_w.rearrange("(k p) e -> p k e", p=P)).then_inc(router_loaded, 16)
            sp.dma_start(iota_in[:, :], iota).then_inc(router_loaded, 16)

            load_unit(0, 1)
            with sp.Fori(1, ITER) as i:
                for b in range(2):
                    load_unit(i, b)

            def load_wq(g):
                wait_past(sp, wq_split, 2 * g)
                sp.dma_start(wq32, wq[:, bass.ds(g * (GROUP * HD), GROUP * HD)].rearrange("(k p) n -> p k n", p=P)).then_inc(wq_loaded, 16)

            def load_wo(g):
                wait_past(sp, wo_split, 2 * g)
                sp.dma_start(wo32, wo[bass.ds(g * (GROUP * HD), GROUP * HD), :].rearrange("(h p) n -> p h n", p=P)).then_inc(wo_loaded, 16)

            sp.wait_ge(factors_applied, 2 * NF * UNITS)
            load_wq(0)
            load_wq(1)
            sp.wait_ge(ln_transposed, 2 * KD)
            load_wo(0)
            load_wq(2)
            with sp.Fori(1, KVH - 2) as g:
                load_wo(g)
                load_wq(g + 2)
            load_wo(KVH - 2)
            load_wo(KVH - 1)
            sp.wait_ge(q_projected, KVH * GROUP)

            def load_expert(e, b):
                wait_past(sp, ew_split, e - 3)
                sp.dma_start(ew32[b], experts[bass.ds(e, 1), :, :].rearrange("a p n -> p (a n)")).then_inc(expert_loaded[b], 16)

            load_expert(0, 0)
            load_expert(1, 1)
            sp.wait_ge(scores_ready, KVH * GROUP * TT)
            load_expert(2, 2)
            load_expert(3, 3)
            with sp.Fori(1, NE // 4) as i:
                for b in range(4):
                    load_expert(4 * i + b, b)
            for t in range(TT):
                sp.wait_ge(moe_added, TT * (NE - 1) + t + 1)
                sp.dma_start(out[t * P:(t + 1) * P, :], x_res[:, t, :]).then_inc(stored, 16)
            sp.wait_ge(stored, 16 * TT)

        @block.gpsimd
        def _(pool):
            step = Steps(pool, pool_step)
            for m in (ident, ident16):
                step.did(pool.memset(m[:, :], 0.0))
            pool.memset(ones16[:, :], 1.0).then_inc(consts_ready, 1)
            pool.memset(ones[:, :], 1.0).then_inc(consts_ready, 1)
            pool.memset(combine[:, :, 0:SHARED], INV).then_inc(consts_ready, 1)
            for f, (b, _) in enumerate(NF4_FACTORS):
                pool.memset(factor_b[:, f:f + 1], b).then_inc(consts_ready, 1)
            step.wait()
            for m in (ident, ident16):
                pool.affine_select(out=m[:, :], in_=m[:, :], compare_op=ALU.not_equal, fill=1.0, base=0,
                                   pattern=[[-1, P]], channel_multiplier=1).then_inc(consts_ready, 1)
            pool.memset(turn[:, 1:2], 0.0).then_inc(turn_set, 1)
            pool.wait_ge(turn_set, 1)

            def scale_codes(i, b):
                u = 2 * i + b
                wait_past(pool, codes_scaled, u)
                pool.wait_ge(codes_loaded[b], 16 * (i + 1))
                pool.tensor_tensor(turn[:, 0:1], turn[:, 1:2], turn[:, 1:2], ALU.mult)
                pool.tensor_scalar(shifted, code_buf[b], -7.0, 1.0, ALU.add, ALU.mult).then_inc(codes_shifted, 1)
                pool.wait_ge(codes_shifted, u + 1)
                pool.wait_ge(absmax_loaded[b], 16 * (i + 1))
                pool.tensor_tensor(absmax_buf[b], shifted, absmax_buf[b], ALU.mult).then_inc(codes_scaled, 1)

            scale_codes(0, 0)
            for k in range(KD):
                pool.wait_ge(ctxT_hi, k + 1)
                pool.tensor_tensor(ctxT[1][:, k, :], ctxT32[:, k, :], ctxT[0][:, k, :], ALU.subtract).then_inc(ctxT_split, 1)

            def split_weights(ks, w32, parts, hi, split):
                for k in ks:
                    pool.wait_ge(hi, k + 1)
                    n = step.did(pool.tensor_scalar(w32[:, k, :], w32[:, k, :], WSCALE, 1.0, ALU.mult, ALU.mult))
                    step.wait(n)
                    pool.tensor_tensor(parts[1][:, k, :], w32[:, k, :], parts[0][:, k, :], ALU.subtract).then_inc(split, 1)

            split_weights(range(KD), wv32, w_v, wv_hi, wv_split)

            def norm_keys(z):
                pool.wait_ge(k_rstd, z + 1)
                pool.tensor_tensor(k_raw, k_raw, k_r[:, :, None].to_broadcast((P, KVH, HD)), ALU.mult).then_inc(k_normed, 1)

            scale_codes(0, 1)
            split_weights(range(2), wk32, w_k, wk_hi, wk_split)
            scale_codes(1, 0)
            split_weights(range(2, KD), wk32, w_k, wk_hi, wk_split)
            scale_codes(1, 1)
            with pool.Fori(1, ITER - 1) as i:
                scale_codes(i + 1, 0)
                norm_keys(i - 1)
                scale_codes(i + 1, 1)
            with pool.Fori(ITER - 2, CT + TT) as z:
                norm_keys(z)

            with pool.Fori(0, KVH) as g:
                for n in range(STEPS):
                    pool.wait_ge(sum_inverted, g * STEPS + n + 1)
                    pool.tensor_tensor(probs[n % 4], probs[n % 4], inv_sum[:, n % 4:n % 4 + 1].to_broadcast((P, KEYS)), ALU.mult)\
                        .then_inc(probs_normed, 1)

        @block.scalar
        def _(act):
            def copy(o, i, scale, done):
                nc.scalar.activation(o, i, ACT.Copy, scale=scale).then_inc(done, 1)

            act.wait_ge(quant_ready, 1)
            def ctx_to_quants(b):
                act.wait_ge(ctx_loaded[b], 16)
                v = ctx32[:, b * KD:(b + 1) * KD, :]
                nc.scalar.activation(v, v, ACT.Identity, scale=qp[:, 1:2], bias=quant_in[:, 3:4]).then_inc(ctx_affine, 1)

            ctx_to_quants(0)
            for t in range(TT):
                act.wait_ge(x_normed, t + 1)
                nc.scalar.activation(xn[:, t, :], xn[:, t, :], ACT.Identity, scale=qp[:, 0:1], bias=quant_in[:, 1:2]).then_inc(x_affine, 1)
            ctx_to_quants(1)

            def squares(i, b, factors):
                u = 2 * i + b
                for f in factors:
                    if f == 0:
                        act.wait_ge(codes_loaded[b], 16 * (i + 1))
                    wait_past(act, factors_applied, 2 * (NF * u + f - 1))
                    nc.scalar.activation(square_buf[(NF * b + f) % 2], code_buf[b], ACT.Square, scale=0.25,
                                         bias=factor_b[:, f:f + 1]).then_inc(squares_ready, 1)

            def activate_gate(u):
                act.wait_ge(gate_done, u + 1)
                nc.scalar.activation(gate_act, GATE, ACT.Silu, scale=NF4_LEAD).then_inc(gate_activated, 1)

            def values_hi(z, dst, banks):
                for h in range(2):
                    act.wait_ge(v_projected, 2 * z + h + 1)
                    copy(dst(h), banks[h], INV, v_hi)

            def copy_keys(z):
                for h in range(2):
                    act.wait_ge(k_projected, 2 * z + h + 1)
                    wait_past(act, k_transposed, 2 * z)
                    copy(k_raw[:, 4 * h:4 * h + 4, :], (KV0, KV1)[h].rearrange("p (a b) -> p a b", a=4), INV, k_copied)
                act.wait_ge(k_copied, 2 * z + 2)
                nc.scalar.activation(k_sq, k_raw, ACT.Square).then_inc(k_squared, 1)

            def keys_hi(z, dst, banks):
                for h in range(2):
                    act.wait_ge(k_transposed, 2 * z + h + 1)
                    nc.scalar.activation(dst(h), banks[h].rearrange("p (a b) -> p a b", a=4), ACT.Copy,
                                         scale=w_qk[:, 0:1]).then_inc(k_hi, 1)

            def pair(i):
                n = i if isinstance(i, int) else 2
                if n > 0:
                    squares(i, 0, range(0, 2))
                    values_hi(i - 1, ctx_values(0, i - 1), (KV0, KV1))
                    squares(i, 0, range(2, 4))
                    activate_gate(2 * i - 1)
                    squares(i, 0, range(4, 5))
                if n > 1:
                    keys_hi(i - 2, ctx_keys(0, i - 2), (KV0, KV1))
                if n > 0:
                    squares(i, 0, range(5, NF))
                squares(i, 1, range(0, 3))
                if n > 0:
                    copy_keys(i - 1)
                squares(i, 1, range(3, 4))
                activate_gate(2 * i)
                squares(i, 1, range(4, NF))

            act.wait_ge(consts_ready, 3 + NF)
            squares(0, 0, range(0, 1))
            for k in range(KD):
                act.wait_ge(x_qT_psum, k + 1)
                copy(x_qT[:, k, :], bank[4 + k][:, 0:TOK // 2].bitcast(bf16), 1.0, x_qT_ready)
            squares(0, 0, range(1, 2))
            act.wait_ge(ctxT_loaded, 16)
            for k in range(KD):
                copy(ctxT[0][:, k, :], ctxT32[:, k, :], 1.0, ctxT_hi)
            squares(0, 0, range(2, 3))
            act.wait_ge(wv_loaded, 16)
            for k in range(KD):
                copy(w_v[0][:, k, :], wv32[:, k, :], WSCALE, wv_hi)
            act.wait_ge(wk_loaded, 16)
            for k in range(KD):
                copy(w_k[0][:, k, :], wk32[:, k, :], WSCALE, wk_hi)
            squares(0, 0, range(3, 4))
            for k in range(0, KD, 2):
                act.wait_ge(ln_transposed, k + 1)
                copy(xnT32[:, k, :], LN_BANK0[k], 1.0, ln_hi)
            squares(0, 0, range(4, NF))
            pair(0)
            pair(1)
            with act.Fori(2, ITER) as i:
                pair(i)
            z = ITER - 1
            values_hi(z, ctx_values(0, z), (KV0, KV1))
            activate_gate(UNITS - 1)
            keys_hi(z - 1, ctx_keys(0, z - 1), (KV0, KV1))
            copy_keys(z)
            values_hi(z + 1, ctx_values(0, z + 1), (GATE, UP))
            for k in range(KD):
                act.wait_ge(ln_transposed, KD + k + 1)
                copy(xnT[0][:, k, :], LN_BANK1[k], 1.0, ln_hi)
            keys_hi(z, ctx_keys(0, z), (bank[0], bank[1]))
            copy_keys(z + 1)

            def half_hi(parts, w32, half, done):
                k = slice(half * 2, half * 2 + 2)
                copy(parts[0][:, k, :], w32[:, k, :], WSCALE, done)

            def wq_part(g, half):
                act.wait_ge(wq_loaded, 16 * (g + 1))
                wait_past(act, q_projected, GROUP * g)
                half_hi(w_q, wq32, half, wq_hi)

            wq_part(0, 0)
            wq_part(0, 1)
            for t in range(TT):
                z = CT + t
                values_hi(z, own_values(0, t), (GATE, UP))
                keys_hi(z - 1, own_keys(0, t - 1) if t else ctx_keys(0, z - 1), (bank[0], bank[1]))
                copy_keys(z)
            def query_out(g, h, src):
                act.wait_ge(q_projected, GROUP * g + h + 1)
                copy(queries(g, 0, h), src, INV, q_hi)
                wait_past(act, q_sumsq, 2 * g + h // 2)
                nc.scalar.activation(q_sq[:, h % 2, :], src, ACT.Square, scale=INV).then_inc(q_squared, 1)

            for h in range(GROUP):
                query_out(0, h, Q0_BANK[h])
                if h == 1:
                    keys_hi(z, own_keys(0, TT - 1), (bank[0], bank[1]))

            wq_part(1, 0)
            wq_part(1, 1)

            def transposed_hi(N, n):
                for c in range(2):
                    act.wait_ge(probs_transposed, 2 * N + c + 1)
                    copy(PT_slot(0, n, c), PT_BANK[c][:, 0:3 * P].rearrange("p (a b) -> p a b", a=3), 1.0, PT_hi)

            def out_hi(S, s, o=O_BANK):
                act.wait_ge(o_done, S + 1)
                copy(OT[s % 2][0], o.rearrange("p (a b) -> p a b", a=GROUP), 1.0, o_hi)

            def expert_hi(e, b):
                act.wait_ge(expert_loaded[b], loaded_after(e, b))
                copy(e_w[b][0], ew32[b], WSCALE, ew_hi)

            def attention(g, first=False, has_q=True, has_wq=True):
                for n in range(STEPS):
                    N = g * STEPS + n
                    if not first or n >= LAG:
                        transposed_hi(N - LAG, (n - LAG) % STEPS)
                    S = due(g, n, OUT, first)
                    if S is not None:
                        out_hi(S, (n - OUT) // GROUP)
                    if n % GROUP == 3 and has_q:
                        query_out(g + 1, n // GROUP, PROJ)
                    act.wait_ge(neg_max_ready, N + 1)
                    if not first or n >= 4:
                        act.wait_ge(probs_transposed, 2 * (N - 3))
                    h, s = n % GROUP, n // GROUP
                    nc.scalar.activation(probs[n % 4], SCORE[n % 2], ACT.Exp, scale=rq_now[:, h * TT + s:h * TT + s + 1],
                                         bias=neg_max[:, n % 4:n % 4 + 1], accum_out=row_sum[:, n % 4:n % 4 + 1])\
                        .then_inc(probs_ready, 1)
                    if n in (9, 10):
                        act.wait_ge(wo_loaded, 16 * (g + 1))
                        wait_past(act, o_projected, g * TT)
                        half_hi(w_o, wo32, n - 9, wo_hi)
                    if n == 15 and has_wq:
                        wq_part(g + 2, 0)
                    if n == 0 and has_q and not first:
                        wq_part(g + 1, 1)
                    if n in (7, 13) and not has_q:
                        expert_hi(n // 8, n // 8)

            attention(0, first=True)
            with act.Fori(1, KVH - 2) as g:
                attention(g)
            attention(KVH - 2, has_wq=False)
            attention(KVH - 1, has_q=False, has_wq=False)
            N = KVH * STEPS
            for n in range(LAG):
                transposed_hi(N - LAG + n, STEPS - LAG + n)
            out_hi(KVH * TT - 2, 0)
            out_hi(KVH * TT - 1, 1, LAST_O)

            for k in range(KD):
                act.wait_ge(ln_transposed, 2 * KD + k + 1)
                copy(xnT[0][:, k, :], LN_BANK2[k], 1.0, ln_hi)
            def expert(e, c, split=True):
                act.wait_ge(e_gate_done, e + 1)
                nc.scalar.activation(e_gate[c % 2], bank[4 + 2 * (c % 2)], ACT.Silu, scale=INV).then_inc(e_gate_act, 1)
                act.wait_ge(e_h_ready, e + 1)
                copy(e_hT[c % 2][0], e_h[c % 2], 1.0, e_h_hi)
                if split:
                    b = (c + 2) % 4
                    act.wait_ge(expert_loaded[b], loaded_after(e + 2, b))
                    copy(e_w[b][0], ew32[b], WSCALE, ew_hi)

            expert(0, 0)
            act.wait_ge(router_shifted, 2)
            for t in range(TT):
                nc.scalar.activation(rprob[:, t, :], logits[:, t, :], ACT.Exp, bias=r_neg[:, t:t + 1],
                                     accum_out=r_sum[:, t:t + 1]).then_inc(router_exp, 1)
            expert(1, 1)
            with act.Fori(0, (NE - 4) // 4) as i:
                for c in range(4):
                    expert(4 * i + 2 + c, (2 + c) % 4)
            for e in range(NE - 2, NE):
                expert(e, e % 4, split=False)

        @block.tensor
        def _(pe):
            def product(o, lhs, rhs, ks, done=None, first=True, last=True, wait_for=lambda k: None):
                n, total = 0, len(ks) * len(PARTS)
                for k in ks:
                    wait_for(k)
                    for a, b in PARTS:
                        m = nc.tensor.matmul(o, lhs(a, k), rhs(b, k), start=first and n == 0, stop=last and n == total - 1)
                        n += 1
                if done is not None:
                    m.then_inc(done, 1)

            def transpose_ln(banks, normed, early=0):
                pe.wait_ge(x_normed, normed + (early or TT))
                for k in range(KD):
                    for t in range(early):
                        nc.tensor.transpose(banks[k][:, t * P:(t + 1) * P], xn[:, t, k * P:(k + 1) * P], ident[:, :])
                if early:
                    pe.wait_ge(x_normed, normed + TT)
                for k in range(KD):
                    for t in range(early, TT):
                        m = nc.tensor.transpose(banks[k][:, t * P:(t + 1) * P], xn[:, t, k * P:(k + 1) * P], ident[:, :])
                    m.then_inc(ln_transposed, 1)

            pe.wait_ge(consts_ready, 5 + NF)
            pe.wait_ge(x_quantised, 1)
            for k in range(KD):
                o = bank[4 + k][:, 0:TOK // 2].bitcast(bf16)
                for t in range(TT):
                    m = nc.tensor.transpose(o[:, t * P:(t + 1) * P], x_q[:, t, k * P:(k + 1) * P], ident16[:, :])
                m.then_inc(x_qT_psum, 1)
            pe.wait_ge(x_qT_ready, KD)
            for t in range(TT):
                for k in range(KD):
                    m = nc.tensor.matmul(ROWSUM[:, t:t + 1], x_qT[:, k, t * P:(t + 1) * P], ones16[:, 0:1], start=k == 0, stop=k == KD - 1)
            m.then_inc(rowsum_done, 1)
            for b in range(NB):
                pe.wait_ge(ctx_quantised, b + 1)
                for k in range(KD):
                    m = nc.tensor.matmul(bank[4 + b], ones16[:, :], ctx_q[:, b * KD + k, :], start=k == 0, stop=k == KD - 1)
                m.then_inc(colsum_done, 1)
                for t in range(2 * b, 2 * b + 2):
                    for k in range(KD):
                        m = nc.tensor.matmul(bank[t], x_qT[:, k, t * P:(t + 1) * P], ctx_q[:, b * KD + k, :],
                                             start=k == 0, stop=k == KD - 1)
                    m.then_inc(qprod_done, 1)
            transpose_ln(LN_BANK0, TT)

            def gate_up(u, b):
                pe.wait_ge(factors_applied, 2 * NF * (u + 1))
                wait_past(pe, h_ready, u)
                for o, c, done in ((GATE, 0, gate_done), (UP, D, up_done)):
                    for k in range(KD):
                        m = nc.tensor.matmul(o, w0[b][:, c + k * P:c + (k + 1) * P], xnT32[:, k, :], start=k == 0, stop=k == KD - 1)
                    m.then_inc(done, 1)

            def down(u, b):
                pe.wait_ge(h_ready, u + 1)
                first = isinstance(u, int) and u == 0
                for t in range(TT):
                    m = nc.tensor.matmul(DOWN[t], h0[b][:, t * P:(t + 1) * P], w0[b][:, 2 * D:3 * D], start=first, stop=True,
                                         skip_group_check=True)
                m.then_inc(down_done, 1)

            def project_values(z, src, banks, half=None):
                for h in range(2) if half is None else (half,):
                    product(banks[h], src, lambda b, k: w_v[b][:, k, h * 512:(h + 1) * 512], range(KD), v_projected)

            def project_keys(z, src):
                for h in range(2):
                    product((KV0, KV1)[h], src, lambda b, k: w_k[b][:, k, h * 512:(h + 1) * 512], range(KD), k_projected)

            def transpose_keys(z, banks):
                pe.wait_ge(k_normed, z + 1)
                for h in range(2):
                    for a in range(4):
                        m = nc.tensor.transpose(banks[h][:, a * P:(a + 1) * P], k_raw[:, 4 * h + a, :], ident[:, :])
                    m.then_inc(k_transposed, 1)

            def ctx_rows(z):
                return lambda a, k: ctxT[a][:, k, bass.ds(z * P, P)]

            def own_rows(t):
                return lambda a, k: xnT[a][:, k, t * P:(t + 1) * P]

            def pair(i, first):
                if first:
                    for done in (ctxT_hi, ctxT_split, wv_hi, wv_split):
                        pe.wait_ge(done, KD)
                    project_values(i, ctx_rows(i), (KV0, KV1))
                gate_up(2 * i, 0)
                if not first:
                    pe.wait_ge(k_copied, 2 * i)
                    project_values(i, ctx_rows(i), (KV0, KV1), 0)
                down(2 * i, 0)
                if not first:
                    project_values(i, ctx_rows(i), (KV0, KV1), 1)
                gate_up(2 * i + 1, 1)
                pe.wait_ge(v_hi, 2 * i + 2)
                pe.wait_ge(v_split, 2 * i + 2)
                if not first:
                    transpose_keys(i - 1, (KV0, KV1))
                down(2 * i + 1, 1)
                if first:
                    for done in (wk_hi, wk_split):
                        pe.wait_ge(done, KD)
                wait_past(pe, k_hi, 2 * i)
                wait_past(pe, k_split, 2 * i)
                project_keys(i, ctx_rows(i))

            pe.wait_ge(ln_hi, 2)
            pe.wait_ge(ln_ready, 2)
            pair(0, True)
            with pe.Fori(1, ITER) as i:
                pair(i, False)
            z = ITER
            project_values(z, ctx_rows(z), (GATE, UP))
            pe.wait_ge(v_hi, 2 * z + 2)
            pe.wait_ge(v_split, 2 * z + 2)
            transpose_ln(LN_BANK1, 2 * TT)
            pe.wait_ge(k_copied, 2 * z)
            project_keys(z, ctx_rows(z))
            transpose_keys(z - 1, (bank[0], bank[1]))
            pe.wait_ge(ln_hi, 2 + KD)
            pe.wait_ge(ln_ready, 2 + KD)
            for t in range(TT):
                z = CT + t
                wait_past(pe, v_hi, 2 * z)
                wait_past(pe, v_split, 2 * z)
                project_values(z, own_rows(t), (GATE, UP))
                pe.wait_ge(k_copied, 2 * z)
                project_keys(z, own_rows(t))
                pe.wait_ge(k_hi, 2 * z - 2)
                pe.wait_ge(k_split, 2 * z - 2)
                transpose_keys(z - 1, (bank[0], bank[1]))
            def project_queries(h, o, wait_for=lambda k: None):
                product(o, lambda a, k: w_q[a][:, k, h * HD:(h + 1) * HD], lambda b, k: xnT[b][:, k, :], range(KD), q_projected,
                        wait_for=wait_for)

            def queries_read(count):
                for done in (q_hi, q_squared, q_split):
                    pe.wait_ge(done, count)

            def sum_squares(g, pair_):
                pe.wait_ge(q_squared, GROUP * g + 2 * pair_ + 2)
                wait_past(pe, sumsq_read, 2 * g + pair_)
                for h in range(2 * pair_, 2 * pair_ + 2):
                    for t in range(TT):
                        c = h * TT + t
                        m = nc.tensor.matmul(SUMSQ[:, c:c + 1], q_sq[:, h % 2, t * P:(t + 1) * P], ones[:, :], start=True, stop=True)
                m.then_inc(q_sumsq, 1)

            pe.wait_ge(wq_hi, 2)
            pe.wait_ge(wq_split, 2)
            pe.wait_ge(k_copied, 2 * (CT + TT))
            for h in range(3):
                project_queries(h, Q0_BANK[h])
            pe.wait_ge(k_hi, 2 * z)
            pe.wait_ge(k_split, 2 * z)
            transpose_keys(z, (bank[0], bank[1]))
            pe.wait_ge(v_hi, 2 * (z + 1))
            pe.wait_ge(v_split, 2 * (z + 1))
            sum_squares(0, 0)
            project_queries(3, Q0_BANK[3])
            for done in (k_hi, k_split, v_hi, v_split):
                pe.wait_ge(done, 2 * (CT + TT))

            def score(g, n):
                h, s = n % GROUP, n // GROUP
                b, N = s // 2, g * STEPS + n
                wait_past(pe, probs_ready, N - 1)
                if s == 0:
                    pe.wait_ge(q_hi, GROUP * g + h + 1)
                    pe.wait_ge(q_split, GROUP * g + h + 1)
                o, parts = SCORE[n % 2], len(PARTS)
                for p, (qa, kb) in enumerate(PARTS):
                    q = queries(g, qa, h, s)
                    nc.tensor.matmul(o[:, 0:CTX], q, key_head(KTc[kb], g, b * CTX, CTX), start=p == 0, stop=p == parts - 1)
                    m = nc.tensor.matmul(o[:, CTX:KEYS], q, key_head(KTl[kb], g, b * (KEYS - CTX), KEYS - CTX),
                                         start=p == 0, stop=p == parts - 1)
                m.then_inc(scores_ready, 1)

            def key_head(keys, g, start, size):
                return keys[:, bass.ds(g, 1), start:start + size].rearrange("p a n -> p (a n)")

            def transpose_probs(N, n):
                pe.wait_ge(probs_normed, N + 1)
                for c in range(2):
                    wait_past(pe, PT_hi, 2 * N + c - 1)
                    wait_past(pe, PT_split, 2 * N + c - 1)
                    for a in range(3):
                        k = 3 * c + a
                        m = nc.tensor.transpose(PT_BANK[c][:, a * P:(a + 1) * P], probs[n % 4][:, k * P:(k + 1) * P], ident[:, :])
                    m.then_inc(probs_transposed, 1)

            def attend(g, S, s, half, o=O_BANK):
                b = s // 2
                if half == 0:
                    if o is O_BANK:
                        wait_past(pe, o_hi, S)
                        wait_past(pe, o_split, S)
                    pe.wait_ge(PT_hi, 2 * GROUP * (S + 1))
                    pe.wait_ge(PT_split, 2 * GROUP * (S + 1))

                def value(a, k):
                    v = Vc[a][:, b * KD + k, :] if k < KD else Vl[a][:, b * 2 + k - KD, :]
                    return v[:, bass.ds(g * HD, HD)]

                product(o, value, lambda c, k: PT[s % 2][c][:, k, :], range(3 * half, 3 * half + 3),
                        o_done if half else None, first=half == 0, last=half == 1)

            def project_out(g, S, s, o=PROJ):
                pe.wait_ge(o_hi, S + 1)
                pe.wait_ge(o_split, S + 1)

                def weights_split(h):
                    if s == 0 and h % 2 == 0:
                        pe.wait_ge(wo_hi, 2 * g + h // 2 + 1)
                        pe.wait_ge(wo_split, 2 * g + h // 2 + 1)

                product(o, lambda a, h: OT[s % 2][a][:, h, :], lambda b, h: w_o[b][:, h, :], range(GROUP), o_projected,
                        wait_for=weights_split)

            def attention(g, first=False, has_q=True):
                for n in range(STEPS):
                    N = g * STEPS + n
                    if n == 0:
                        wait_past(pe, PT_split, 2 * (N - 1 - LAG) + 1)
                        sum_squares(g, 1)
                    if n == 9 and has_q:
                        pe.wait_ge(PT_split, 2 * (N - 1 - LAG) + 1)
                        sum_squares(g + 1, 0)
                    if not first or n >= LAG:
                        if n == 1 or (n == 10 and has_q):
                            wait_past(pe, sumsq_read, 2 * g + 2 if n == 1 else 2 * g + 3)
                        transpose_probs(N - LAG, (n - LAG) % STEPS)
                    score(g, n)
                    S = due(g, n, VALUES_0, first)
                    if S is not None:
                        attend(g if n >= VALUES_0 else g - 1, S, (n - VALUES_0) // GROUP % TT, 0)
                    S = due(g, n, VALUES_1, first)
                    if S is not None:
                        attend(g if n >= VALUES_1 else g - 1, S, (n - VALUES_1) // GROUP % TT, 1)
                    S = due(g, n, WO, first)
                    if S is not None:
                        queries_read(GROUP * (g + 1) + n // GROUP if has_q else KVH * GROUP)
                        wait_past(pe, attn_added, S)
                        project_out(g if n >= WO else g - 1, S, (n - WO) // GROUP % TT)
                    if n % GROUP == 2 and has_q:
                        h = n // GROUP

                        def weights_split(k):
                            if h == 0 and k % 2 == 0:
                                pe.wait_ge(wq_hi, 2 * (g + 1) + k // 2 + 1)
                                pe.wait_ge(wq_split, 2 * (g + 1) + k // 2 + 1)

                        if first and n < WO:
                            queries_read(GROUP * (g + 1) + h)
                        else:
                            pe.wait_ge(attn_added, g * TT + (n - WO + 2) // GROUP)
                        project_queries(h, PROJ, weights_split)

            attention(0, first=True)
            with pe.Fori(1, KVH - 1) as g:
                attention(g)
            attention(KVH - 1, has_q=False)
            N, S = KVH * STEPS, KVH * TT
            for n in range(LAG):
                transpose_probs(N - LAG + n, STEPS - LAG + n)
            pe.wait_ge(attn_added, S - 3)
            project_out(KVH - 1, S - 3, 1)
            attend(KVH - 1, S - 2, 2, 1)
            pe.wait_ge(probs_ready, N)
            for half in range(2):
                attend(KVH - 1, S - 1, 3, half, LAST_O)
            pe.wait_ge(attn_added, S - 2)
            project_out(KVH - 1, S - 2, 2)
            project_out(KVH - 1, S - 1, 3, LAST_PROJ)

            pe.wait_ge(attn_added, KVH * TT - 1)
            transpose_ln(LN_BANK2, 3 * TT, early=2)

            def route():
                for t in range(TT):
                    product(bank[0][:, t * EXPERTS:(t + 1) * EXPERTS], lambda a, k: xnT[a][:, k, t * P:(t + 1) * P],
                            lambda b, k: r_w[b][:, k, :], range(KD), logits_done)

            def expert_in(e, c):
                pe.wait_ge(ew_hi, e + 1)
                pe.wait_ge(ew_split, e + 1)
                wait_past(pe, e_h_ready, e - 1)
                for j, done in ((0, e_gate_done), (1, e_up_done)):

                    def input_split(k):
                        if isinstance(e, int) and e == 0 and j == 0:
                            pe.wait_ge(ln_hi, 2 + KD + k + 1)
                            pe.wait_ge(ln_ready, 2 + KD + k + 1)

                    product(bank[4 + 2 * (c % 2) + j], lambda a, k: e_w[c][a][:, k * 2 * P + j * P:k * 2 * P + (j + 1) * P],
                            lambda b, k: xnT[b][:, k, :], range(KD), done, wait_for=input_split)

            def expert_out(e, c):
                pe.wait_ge(e_h_hi, e + 1)
                pe.wait_ge(e_h_split, e + 1)
                for t in range(TT):
                    wait_past(pe, moe_added, TT * (e - 1) + t + 1 if not isinstance(e, int) or e > 0 else 0)
                    product(bank[t], lambda a, k: e_hT[c % 2][a][:, t * P:(t + 1) * P], lambda b, k: e_w[c][b][:, 2 * D:3 * D],
                            range(1), e_down_done)

            expert_in(0, 0)
            route()
            expert_in(1, 1)
            pe.wait_ge(logits_read, 1)
            expert_out(0, 0)
            with pe.Fori(0, (NE - 4) // 4) as i:
                for c in range(4):
                    e = 4 * i + 2 + c
                    expert_in(e, (2 + c) % 4)
                    expert_out(e - 1, (1 + c) % 4)
            for e in range(NE - 2, NE):
                expert_in(e, e % 4)
                expert_out(e - 1, (e - 1) % 4)
            expert_out(NE - 1, (NE - 1) % 4)

        @block.vector
        def _(dve):
            step = Steps(dve, dve_step)
            vec = nc.vector

            def rsqrt(y, v, t, done):
                n = step.did(vec.tensor_scalar(t.bitcast(i32), v.bitcast(i32), 1, None, ALU.logical_shift_right))
                yield
                step.wait(n)
                n = step.did(vec.tensor_scalar(y.bitcast(i32), t.bitcast(i32), -1.0, RSQRT_SEED, ALU.mult, ALU.add))
                for r in range(3):
                    yield
                    step.wait(n)
                    n = step.did(vec.scalar_tensor_tensor(t, y, -0.5, y, ALU.mult, ALU.mult))
                    yield
                    step.wait(n)
                    n = step.did(vec.tensor_tensor(t, t, v, ALU.mult))
                    yield
                    step.wait(n)
                    if r < 2:
                        n = step.did(vec.scalar_tensor_tensor(y, t, 1.5, y, ALU.add, ALU.mult))
                vec.scalar_tensor_tensor(y, t, 1.5, y, ALU.add, ALU.mult).then_inc(done, 1)

            def run(steps):
                for _ in steps:
                    pass

            ln_rstd = 0

            def layernorm(tiles=range(TT)):
                c = slice(tiles[0], tiles[-1] + 1)
                n = [step.did(vec.bn_stats(bn[:, t, :], x_res[:, t, :])) for t in tiles]
                for t in tiles:
                    step.wait(n[t - tiles[0]])
                    last = step.did(vec.bn_aggr(mv[:, t, :], bn[:, t, :]))
                step.wait(last)
                n = step.did(vec.tensor_scalar(ln_v[:, c], mv[:, c, 1], LN_EPS, None, ALU.add))
                step.wait(n)
                run(rsqrt(ln_r[:, c], ln_v[:, c], ln_t[:, c], ln_rstd_ready))
                nonlocal ln_rstd
                ln_rstd += 1
                dve.wait_ge(ln_rstd_ready, ln_rstd)
                for t in tiles:
                    vec.tensor_scalar(xn[:, t, :], x_res[:, t, :], mv[:, t, 0:1], ln_r[:, t:t + 1], ALU.subtract, ALU.mult)\
                        .then_inc(x_normed, 1)

            def apply_factor(i, b, f):
                u = 2 * i + b
                dve.wait_ge(squares_ready, NF * u + f + 1)
                if f == 0:
                    dve.wait_ge(codes_scaled, u + 1)
                    wait_past(dve, down_done, u - 1)
                for c in range(2):
                    r = slice(c * HALF, (c + 1) * HALF)
                    if f > 0:
                        dve.wait_ge(factors_applied, 2 * (NF * u + f - 1) + c + 1)
                    vec.scalar_tensor_tensor(w0[b][:, r], square_buf[(NF * b + f) % 2][:, r], NF4_FACTORS[f][1],
                                             w0[b][:, r] if f else absmax_buf[b][:, r], ALU.add, ALU.mult)\
                        .then_inc(factors_applied, 1)

            dve.wait_ge(quant_loaded, 64)
            step.did(vec.reciprocal(qp[:, 0:1], quant_in[:, 0:1]))
            step.did(vec.reciprocal(qp[:, 1:2], quant_in[:, 2:3]))
            step.did(vec.tensor_scalar(qp[:, 2:3], quant_in[:, 1:2], -1.0, 128.0, ALU.mult, ALU.add))
            step.did(vec.tensor_scalar(qp[:, 3:4], quant_in[:, 3:4], -1.0, 128.0, ALU.mult, ALU.add))
            step.did(vec.tensor_tensor(qp[:, 4:5], quant_in[:, 0:1], quant_in[:, 2:3], ALU.mult))
            step.wait()
            n = step.did(vec.tensor_tensor(qp[:, 6:7], qp[:, 2:3], qp[:, 3:4], ALU.mult))
            step.wait(n)
            vec.tensor_scalar(qp[:, 5:6], qp[:, 6:7], float(D), None, ALU.mult).then_inc(quant_ready, 1)
            dve.wait_ge(x_loaded, 16)
            layernorm()

            def quantise(o, v, done):
                n = step.did(vec.tensor_scalar(v, v, ROUND, ROUND, ALU.add, ALU.max))
                step.wait(n)
                vec.tensor_scalar(o, v, ROUND + 255.0, ROUND + 128.0, ALU.min, ALU.subtract).then_inc(done, 1)

            dve.wait_ge(ctx_affine, 1)
            quantise(ctx_q[:, 0:KD, :], ctx32[:, 0:KD, :], ctx_quantised)
            dve.wait_ge(x_affine, TT)
            quantise(x_q, xn, x_quantised)
            dve.wait_ge(ctx_affine, 2)
            quantise(ctx_q[:, KD:2 * KD, :], ctx32[:, KD:2 * KD, :], ctx_quantised)
            apply_factor(0, 0, 0)
            dve.wait_ge(quant_ready, 1)
            dve.wait_ge(rowsum_done, 1)
            n_row = step.did(vec.tensor_scalar(row_term[:, :], ROWSUM, qp[:, 3:4], qp[:, 5:6], ALU.mult, ALU.add))
            step.wait(n_row)
            for b in range(NB):
                dve.wait_ge(colsum_done, b + 1)
                n_col = step.did(vec.tensor_scalar(xn[:, b, :], bank[4 + b], qp[:, 2:3], None, ALU.mult))
                for t in range(2 * b, 2 * b + 2):
                    dve.wait_ge(qprod_done, t + 1)
                    step.wait(n_col)
                    v = xn[:, 2 + t % 2, :]
                    if b:
                        step.wait(n_add[t % 2])
                    else:
                        n_add = [0, 0]
                    n = step.did(vec.scalar_tensor_tensor(v, bank[t], row_term[:, t:t + 1], xn[:, b, :], ALU.add, ALU.add))
                    step.wait(n)
                    n_add[t % 2] = step.did(vec.scalar_tensor_tensor(x_res[:, t, :], v, qp[:, 4:5], x_res[:, t, :], ALU.mult, ALU.add))
            step.wait()
            layernorm()
            apply_factor(0, 0, 1)
            apply_factor(0, 0, 2)
            for k in range(1, KD, 2):
                dve.wait_ge(ln_transposed, k + 1)
                vec.tensor_copy(xnT32[:, k, :], LN_BANK0[k]).then_inc(ln_ready, 1)
            for f in range(3, NF):
                apply_factor(0, 0, f)

            def activate(u, b):
                dve.wait_ge(gate_activated, u + 1)
                dve.wait_ge(up_done, u + 1)
                vec.scalar_tensor_tensor(h0[b], UP, NF4_LEAD, gate_act, ALU.mult, ALU.mult).then_inc(h_ready, 1)

            def values_lo(z, hi, lo, banks):
                for h in range(2):
                    dve.wait_ge(v_hi, 2 * z + h + 1)
                    vec.scalar_tensor_tensor(lo(h), banks[h], INV, hi(h), ALU.mult, ALU.subtract).then_inc(v_split, 1)

            def key_rms(z):
                dve.wait_ge(k_squared, z + 1)
                n = step.did(vec.tensor_reduce(k_ss[:, :], k_sq, AX, ALU.add))
                yield
                step.wait(n)
                n = step.did(vec.tensor_scalar(k_v[:, :], k_ss[:, :], 1.0 / HD, RMS_EPS, ALU.mult, ALU.add))
                yield
                step.wait(n)
                yield from rsqrt(k_r[:, :], k_v[:, :], k_t[:, :], k_rstd)

            def keys_lo(z, hi, lo, banks):
                for h in range(2):
                    dve.wait_ge(k_hi, 2 * z + h + 1)
                    vec.scalar_tensor_tensor(lo(h), banks[h].rearrange("p (a b) -> p a b", a=4), w_qk[:, 0:1], hi(h),
                                             ALU.mult, ALU.subtract).then_inc(k_split, 1)

            def pair(i):
                n = i if isinstance(i, int) else 2
                if n > 0:
                    for f in range(NF):
                        apply_factor(i, 0, f)
                        if f == 0:
                            values_lo(i - 1, ctx_values(0, i - 1), ctx_values(1, i - 1), (KV0, KV1))
                        if f == 2:
                            activate(2 * i - 1, 1)
                        if f == 4 and n > 1:
                            keys_lo(i - 2, ctx_keys(0, i - 2), ctx_keys(1, i - 2), (KV0, KV1))
                norm = key_rms(i - 1) if n > 0 else iter(())
                for f in range(NF):
                    apply_factor(i, 1, f)
                    if f == 3:
                        activate(2 * i, 0)
                    if f > 1:
                        for _ in range(3):
                            next(norm, None)
                run(norm)

            dve.wait_ge(norms_loaded, 16)
            vec.tensor_tensor(w_qk[:, :], norm_in[:, 0:1], norm_in[:, 1:2], ALU.mult).then_inc(w_qk_ready, 1)
            dve.wait_ge(router_loaded, 32)
            n = step.did(vec.tensor_scalar(r_w[0][:, :, :], rw32[:, :, :], WSCALE, None, ALU.mult))
            step.wait(n)
            step.did(vec.scalar_tensor_tensor(r_w[1][:, :, :], rw32[:, :, :], WSCALE, r_w[0][:, :, :], ALU.mult, ALU.subtract))
            pair(0)
            pair(1)
            base = step.base + step.k
            step.at(base)
            PER_PAIR = 12
            with dve.Fori(2, ITER) as i:
                step.at((i - 2) * PER_PAIR + base)
                pair(i)
                assert step.k == PER_PAIR, step.k
            step.at(base + (ITER - 2) * PER_PAIR)
            z = ITER - 1
            values_lo(z, ctx_values(0, z), ctx_values(1, z), (KV0, KV1))
            activate(UNITS - 1, 1)
            keys_lo(z - 1, ctx_keys(0, z - 1), ctx_keys(1, z - 1), (KV0, KV1))
            dve.wait_ge(down_done, UNITS)
            for t in range(TT):
                vec.scalar_tensor_tensor(x_res[:, t, :], DOWN[t], NF4_LEAD, x_res[:, t, :], ALU.mult, ALU.add).then_inc(ffn_added, 1)
            dve.wait_ge(ffn_added, TT)
            layernorm()
            values_lo(z + 1, ctx_values(0, z + 1), ctx_values(1, z + 1), (GATE, UP))

            def ln_lo(done, banks):
                for k in range(KD):
                    dve.wait_ge(ln_hi, done + k + 1)
                    vec.tensor_tensor(xnT[1][:, k, :], banks[k], xnT[0][:, k, :], ALU.subtract).then_inc(ln_ready, 1)

            ln_lo(2, LN_BANK1)
            run(key_rms(z))
            keys_lo(z, ctx_keys(0, z), ctx_keys(1, z), (bank[0], bank[1]))
            run(key_rms(z + 1))

            def half_lo(parts, w32, half, done):
                k = slice(half * 2, half * 2 + 2)
                vec.scalar_tensor_tensor(flat(parts[1][:, k, :]), flat(w32[:, k, :]), WSCALE, flat(parts[0][:, k, :]),
                                         ALU.mult, ALU.subtract).then_inc(done, 1)

            def wq_lo(g, half):
                dve.wait_ge(wq_hi, 2 * g + half + 1)
                half_lo(w_q, wq32, half, wq_split)

            def wo_lo(g, half):
                dve.wait_ge(wo_hi, 2 * g + half + 1)
                half_lo(w_o, wo32, half, wo_split)

            wq_lo(0, 0)
            wq_lo(0, 1)
            for t in range(TT):
                z = CT + t
                values_lo(z, own_values(0, t), own_values(1, t), (GATE, UP))
                if t:
                    keys_lo(z - 1, own_keys(0, t - 1), own_keys(1, t - 1), (bank[0], bank[1]))
                else:
                    keys_lo(z - 1, ctx_keys(0, z - 1), ctx_keys(1, z - 1), (bank[0], bank[1]))
                run(key_rms(z))
            def query_lo(g, h, src):
                dve.wait_ge(q_squared, GROUP * g + h + 1)
                vec.scalar_tensor_tensor(queries(g, 1, h), src, INV, queries(g, 0, h), ALU.mult, ALU.subtract).then_inc(q_split, 1)

            def query_rms(g, pair_):
                dve.wait_ge(q_sumsq, 2 * g + pair_ + 1)
                c = slice(pair_ * 2 * TT, (pair_ + 1) * 2 * TT)
                vec.tensor_scalar(rq_v[:, c], SUMSQ[:, c], 1.0 / HD, RMS_EPS, ALU.mult, ALU.add).then_inc(sumsq_read, 1)
                dve.wait_ge(sumsq_read, 2 * g + pair_ + 1)
                return rsqrt(rq_next[:, c], rq_v[:, c], rq_t[:, c], rq_ready)

            def use_query_rms(g, pair_):
                dve.wait_ge(rq_ready, 2 * g + pair_ + 1)
                c = slice(pair_ * 2 * TT, (pair_ + 1) * 2 * TT)
                return step.did(vec.tensor_scalar(rq_now[:, c], rq_next[:, c], HD ** -0.5, None, ALU.mult))

            for h in range(3):
                query_lo(0, h, Q0_BANK[h])
                if h == 1:
                    keys_lo(z, own_keys(0, TT - 1), own_keys(1, TT - 1), (bank[0], bank[1]))
            run(query_rms(0, 0))
            query_lo(0, 3, Q0_BANK[3])

            def row_maximum(N, n, wait_for):
                h, s = n % GROUP, n // GROUP
                dve.wait_ge(scores_ready, N + 1)
                c = slice(n % 4, n % 4 + 1)
                m = step.did(vec.tensor_reduce(row_max[:, c], SCORE[n % 2], AX, ALU.max))
                if wait_for is not None:
                    step.wait(wait_for)
                return m

            def negate_maximum(n, m):
                h, s = n % GROUP, n // GROUP
                c = slice(n % 4, n % 4 + 1)
                step.wait(m)
                vec.tensor_scalar(neg_max[:, c], row_max[:, c], rq_now[:, h * TT + s:h * TT + s + 1], -1.0, ALU.mult, ALU.mult)\
                    .then_inc(neg_max_ready, 1)

            def invert_sum(N, n):
                dve.wait_ge(probs_ready, N + 1)
                c = slice(n % 4, n % 4 + 1)
                vec.reciprocal(inv_sum[:, c], row_sum[:, c]).then_inc(sum_inverted, 1)

            def transposed_lo(N, n):
                for c in range(2):
                    dve.wait_ge(PT_hi, 2 * N + c + 1)
                    vec.tensor_tensor(PT_slot(1, n, c), PT_BANK[c][:, 0:3 * P].rearrange("p (a b) -> p a b", a=3),
                                      PT_slot(0, n, c), ALU.subtract).then_inc(PT_split, 1)

            def out_lo(S, s, o=O_BANK):
                dve.wait_ge(o_hi, S + 1)
                vec.tensor_tensor(flat(OT[s % 2][1]), o, flat(OT[s % 2][0]), ALU.subtract).then_inc(o_split, 1)

            def add_attention(S, s, o=PROJ):
                dve.wait_ge(o_projected, S + 1)
                vec.scalar_tensor_tensor(x_res[:, s, :], o, INV, x_res[:, s, :], ALU.mult, ALU.add).then_inc(attn_added, 1)

            def expert_lo(e, b):
                dve.wait_ge(ew_hi, e + 1)
                vec.scalar_tensor_tensor(e_w[b][1], ew32[b], WSCALE, e_w[b][0], ALU.mult, ALU.subtract).then_inc(ew_split, 1)

            def attention(g, first=False, has_q=True):
                norm = iter(())

                def advance(k=1):
                    for _ in range(k):
                        next(norm, None)

                for n in range(STEPS):
                    N = g * STEPS + n
                    advance()
                    if not first or n:
                        invert_sum(N - 1, (n - 1) % STEPS)
                        advance()
                    if not first or n >= LAG:
                        transposed_lo(N - LAG, (n - LAG) % STEPS)
                    if n == 0:
                        norm = query_rms(g, 1)
                    if n == 9 and has_q:
                        norm = query_rms(g + 1, 0)
                    if n == 2:
                        run(norm)
                    used = use_query_rms(g, n // 2) if n in (0, 2) else None
                    m = row_maximum(N, n, used)
                    advance()
                    negate_maximum(n, m)
                    advance()
                    S = due(g, n, OUT, first)
                    if S is not None:
                        out_lo(S, (n - OUT) // GROUP)
                        advance()
                    if n % GROUP == 3 and has_q:
                        query_lo(g + 1, n // GROUP, PROJ)
                        advance()
                    S = due(g, n, ADD, first)
                    if S is not None:
                        add_attention(S, (n - ADD) // GROUP % TT)
                        advance()
                    if n in (0, 1) and has_q:
                        wq_lo(g + 1, n)
                    if n in (10, 11):
                        wo_lo(g, n - 10)
                    if n == 8 and not has_q:
                        expert_lo(0, 0)
                run(norm)

            attention(0, first=True)
            base = step.base + step.k
            PER_GROUP = STEPS + 2 + 2 * 10
            with dve.Fori(1, KVH - 2) as g:
                step.at((g - 1) * PER_GROUP + base)
                attention(g)
                assert step.k == PER_GROUP, step.k
            step.at(base + (KVH - 3) * PER_GROUP)
            attention(KVH - 2)
            attention(KVH - 1, has_q=False)
            N = KVH * STEPS
            invert_sum(N - 1, STEPS - 1)
            for n in range(LAG):
                transposed_lo(N - LAG + n, STEPS - LAG + n)
            expert_lo(1, 1)
            add_attention(KVH * TT - 3, 1)
            out_lo(KVH * TT - 2, 0)
            dve.wait_ge(wo_split, 2 * KVH)
            dve.wait_ge(attn_added, KVH * TT - 2)
            layernorm(range(2))
            out_lo(KVH * TT - 1, 1, LAST_O)
            add_attention(KVH * TT - 2, 2)
            add_attention(KVH * TT - 1, 3, LAST_PROJ)
            dve.wait_ge(attn_added, KVH * TT)
            layernorm(range(2, TT))
            ln_lo(2 + KD, LN_BANK2)

            def add_expert(e, column):
                for t in range(TT):
                    dve.wait_ge(e_down_done, TT * e + t + 1)
                    wait_past(dve, moe_added, TT * (e - 1) + t + 1 if not isinstance(e, int) or e > 0 else 0)
                    vec.scalar_tensor_tensor(x_res[:, t, :], bank[t], column(t), x_res[:, t, :], ALU.mult, ALU.add)\
                        .then_inc(moe_added, 1)

            def expert(e, c, split=True, add=True):
                dve.wait_ge(e_gate_act, e + 1)
                dve.wait_ge(e_up_done, e + 1)
                vec.scalar_tensor_tensor(e_h[c % 2], bank[5 + 2 * (c % 2)], INV, e_gate[c % 2], ALU.mult, ALU.mult).then_inc(e_h_ready, 1)
                if split:
                    expert_lo(e + 2, (c + 2) % 4)
                dve.wait_ge(e_h_hi, e + 1)
                vec.tensor_tensor(e_hT[c % 2][1], e_h[c % 2], e_hT[c % 2][0], ALU.subtract).then_inc(e_h_split, 1)
                if add:
                    add_expert(e - 1, lambda t: combine[:, t, bass.ds(e - 1, 1)])

            expert(0, 0, add=False)

            dve.wait_ge(logits_done, TT)
            vec.tensor_scalar(logits, bank[0][:, 0:TT * EXPERTS].rearrange("p (t e) -> p t e", t=TT), INV, None, ALU.mult)\
                .then_inc(logits_read, 1)
            dve.wait_ge(logits_read, 1)
            vec.tensor_reduce(r_max[:, :], logits, AX, ALU.max).then_inc(router_shifted, 1)
            dve.wait_ge(router_shifted, 1)
            vec.tensor_scalar(r_neg[:, :], r_max[:, :], -1.0, None, ALU.mult).then_inc(router_shifted, 1)
            dve.wait_ge(router_exp, TT)
            n = step.did(vec.reciprocal(r_inv[:, :], r_sum[:, :]))
            step.wait(n)
            ns = [step.did(vec.tensor_scalar(rprob[:, t, :], rprob[:, t, :], r_inv[:, t:t + 1], None, ALU.mult)) for t in range(TT)]
            nm = []
            for t in range(TT):
                step.wait(ns[t])
                nm.append(step.did(vec.max(out=top8[:, t, :], in_=rprob[:, t, :])))
            for t in range(TT):
                step.wait(nm[t])
                n = step.did(vec.max_index(top8i[:, t, :], top8[:, t, :], rprob[:, t, :]))
            step.did(vec.tensor_tensor(r_sum[:, :], top8[:, :, 0], top8[:, :, 1], ALU.add))
            step.wait()
            step.did(vec.tensor_copy(top_i[:, :, :], top8i[:, :, 0:2]))
            n = step.did(vec.reciprocal(r_max[:, :], r_sum[:, :]))
            step.wait(n)
            n = step.did(vec.tensor_tensor(top_w[:, :, :], top8[:, :, 0:2], r_max[:, :, None].to_broadcast((P, TT, 2)), ALU.mult))
            step.wait(n)
            for t in range(TT):
                for c in range(2):
                    n = step.did(vec.tensor_scalar(pick[:, t, c, :], iota_in[:, :], top_i[:, t, c:c + 1], top_w[:, t, c:c + 1],
                                                   ALU.is_equal, ALU.mult))
            step.wait(n)
            n = step.did(vec.tensor_tensor(logits, pick[:, :, 0, :], pick[:, :, 1, :], ALU.add))
            step.wait(n)
            dve.wait_ge(consts_ready, 3)
            vec.tensor_scalar(combine[:, :, SHARED:NE], logits, INV, None, ALU.mult).then_inc(combine_ready, 1)
            dve.wait_ge(combine_ready, 1)

            expert(1, 1)
            with dve.Fori(0, (NE - 4) // 4) as i:
                for c in range(4):
                    expert(4 * i + 2 + c, (2 + c) % 4)
            for e in range(NE - 2, NE):
                expert(e, e % 4, split=False)
            add_expert(NE - 1, lambda t: combine[:, t, NE - 1:NE])


def kernel(x, ctx_4096, L0_xattn_x1_scale, L0_xattn_x1_zp, L0_xattn_x2_scale, L0_xattn_x2_zp, L0_ffn_gate_q,
           L0_ffn_gate_absmax, L0_ffn_up_q, L0_ffn_up_absmax, L0_ffn_down_q, L0_ffn_down_absmax, L1_xattn_Wq, L1_xattn_Wk,
           L1_xattn_Wv, L1_xattn_Wo, L1_xattn_q_norm_w, L1_xattn_k_norm_w, L1_ffn_gate_w, L1_ffn_w_gate_up, L1_ffn_w_down,
           L1_ffn_shared_w_gate_up, L1_ffn_shared_w_down):
    import numpy as np
    import concourse.bacc as bacc
    from concourse.bass_utils import run_bass_kernel_spmd

    a = np.ascontiguousarray
    f = np.asarray
    ctx = f(ctx_4096).reshape(NB * CTX, D)

    def by_unit(w):
        return f(w).reshape(UNITS, P, KD, P).transpose(0, 3, 2, 1).reshape(UNITS, P, D)

    def by_unit_absmax(s):
        return f(s).reshape(UNITS, P, KD, 2).transpose(0, 3, 2, 1).reshape(UNITS, 2, D)

    codes = np.concatenate([by_unit(L0_ffn_gate_q), by_unit(L0_ffn_up_q),
                            f(L0_ffn_down_q).T.reshape(UNITS, P, D)], axis=2)
    absmax = np.concatenate([by_unit_absmax(L0_ffn_gate_absmax), by_unit_absmax(L0_ffn_up_absmax),
                             f(L0_ffn_down_absmax).reshape(D, UNITS, 2).transpose(1, 2, 0)], axis=2)

    def expert_in(gate, up):
        both = np.stack([gate, up], axis=1).reshape(-1, 2, INTER, KD, P)
        return both.transpose(0, 4, 3, 1, 2).reshape(-1, P, KD * 2 * INTER)

    gu, sgu = f(L1_ffn_w_gate_up), f(L1_ffn_shared_w_gate_up).reshape(2, SHARED, INTER, D)
    experts = np.concatenate([
        np.concatenate([expert_in(sgu[0], sgu[1]), f(L1_ffn_shared_w_down).T.reshape(SHARED, INTER, D)], axis=2),
        np.concatenate([expert_in(gu[:, :INTER], gu[:, INTER:]), f(L1_ffn_w_down).transpose(0, 2, 1)], axis=2)], axis=0)
    ins = [
        ("x", f(x).reshape(TOK, D)),
        ("ctx", ctx),
        ("ctx_t", ctx.T),
        ("quant", np.stack([f(L0_xattn_x1_scale), f(L0_xattn_x1_zp), f(L0_xattn_x2_scale), f(L0_xattn_x2_zp)])),
        ("codes", codes),
        ("absmax", absmax),
        ("wk", f(L1_xattn_Wk)),
        ("wv", f(L1_xattn_Wv)),
        ("wq", f(L1_xattn_Wq)),
        ("wo", f(L1_xattn_Wo)),
        ("norms", np.stack([f(L1_xattn_q_norm_w), f(L1_xattn_k_norm_w)], axis=1)),
        ("router_w", f(L1_ffn_gate_w).T),
        ("experts", experts),
        ("iota", np.tile(np.arange(EXPERTS, dtype=np.float32), (P, 1))),
    ]
    nc = bacc.Bacc("TRN2", target_bir_lowering=False, num_devices=1)
    arrays, args = {}, []
    for name, v in ins:
        v = a(v)
        arrays[name] = v
        args.append(nc.dram_tensor(name, v.shape, mybir.dt.from_np(v.dtype), kind="ExternalInput").ap())
    args.append(nc.dram_tensor("out", (TOK, D), mybir.dt.float32, kind="ExternalOutput").ap())
    bass_xattn_ffn_two_layers(nc, *args)
    r = run_bass_kernel_spmd(nc, [arrays], core_ids=[0])
    return r.results[0]["out"].reshape(NB, TOK // NB, D)
```
